# Optimizing a Trainium2 kernel written in Bass

```python
import numpy as np
import jax
import jax.numpy as jnp

def _softmax(x, axis=-1):
    return jax.nn.softmax(x, axis=axis)

def _gelu(x):
    return jax.nn.gelu(x, approximate=True)

def _silu(x):
    return jax.nn.silu(x)

def _sigmoid(x):
    return jax.nn.sigmoid(x)

def _layernorm(x, axis=-1, eps=1e-05):
    m = jnp.mean(x, axis=axis, keepdims=True)
    v = jnp.var(x, axis=axis, keepdims=True)
    return (x - m) / jnp.sqrt(v + eps)

def _scatter_add(tgt, idx, src, axis=0):
    return tgt.at[idx].add(src)

def _segment_sum(src, seg, n):
    return jax.ops.segment_sum(src, seg, n)
kernel_name = 'mk_gnn_resnorm_d2_gnn_r8_ea219f'

def setup_inputs(seed: int=0):
    np.random.seed(seed)
    _w = jnp.asarray

    def _rec_inputs():
        import jax
        import jax.numpy as jnp
        _gk = jax.random.key(seed)
        x = -0.000202 + 1 * jax.random.normal(jax.random.fold_in(_gk, 1), (6250, 128), jnp.float32)
        _s = jax.random.randint(jax.random.fold_in(_gk, 2), (50000,), 0, 6250, jnp.int32)
        _d = jax.random.randint(jax.random.fold_in(_gk, 3), (50000,), 0, 6250, jnp.int32)
        _loop = jnp.arange(6250, dtype=jnp.int32)
        src = jnp.concatenate([_s, _d, _loop])
        dst = jnp.concatenate([_d, _s, _loop])
        _o = jnp.argsort(dst, stable=True)
        src = src[_o]
        dst = dst[_o]
        edge_type_6 = jax.random.randint(jax.random.fold_in(_gk, 14), (106250,), 0, 6, jnp.int32)
        edge_weight = jax.random.uniform(jax.random.fold_in(_gk, 15), (106250,), jnp.float32, 0.0, 0.999999)
        node_type_4 = jax.random.randint(jax.random.fold_in(_gk, 16), (6250,), 0, 4, jnp.int32)
        return (x, src, dst, edge_type_6, edge_weight, node_type_4)
    x, src, dst, edge_type_6, edge_weight, node_type_4 = _rec_inputs()

    def _L0_gnn_setup():
        import jax, jax.numpy as jnp
        import numpy as np
        N, E, DIM, H, T, R = (6250, 50000, 128, 8, 4, 6)
        D = DIM // H

        def _typed_linear(x, W, types):
            out = jnp.zeros((x.shape[0], W.shape[-1]), x.dtype)
            for t in range(W.shape[0]):
                out = jnp.where((types == t)[:, None], x @ W[t], out)
            return out

        def _typed_rel(xe, W, etype):
            out = jnp.zeros_like(xe)
            for r in range(W.shape[1]):
                yr = jnp.einsum('ehd,hdo->eho', xe, W[:, r])
                out = jnp.where((etype == r)[:, None, None], yr, out)
            return out
        key = jax.random.key(seed)
        ks = jax.random.split(key, 12)
        s = 0.1
        return {'x': jax.random.normal(ks[0], (N, DIM), jnp.float32), 'src': jax.random.randint(ks[1], (E,), 0, N), 'dst': jax.random.randint(ks[2], (E,), 0, N), 'ntype': jax.random.randint(ks[3], (N,), 0, T), 'etype': jax.random.randint(ks[4], (E,), 0, R), 'Wk': jax.random.normal(ks[5], (T, DIM, DIM), jnp.float32) * s, 'Wq': jax.random.normal(ks[6], (T, DIM, DIM), jnp.float32) * s, 'Wv': jax.random.normal(ks[7], (T, DIM, DIM), jnp.float32) * s, 'Wa': jax.random.normal(ks[8], (T, DIM, DIM), jnp.float32) * s, 'rel_pri': jnp.ones((H, R), jnp.float32) + jax.random.normal(ks[9], (H, R), jnp.float32) * 0.1, 'rel_att': jax.random.normal(ks[10], (H, R, D, D), jnp.float32) * 0.25, 'rel_msg': jax.random.normal(ks[11], (H, R, D, D), jnp.float32) * 0.25, 'skip': jnp.ones((T,), jnp.float32), 'ln_gamma': jnp.ones((DIM,), jnp.float32), 'ln_beta': jnp.zeros((DIM,), jnp.float32)}
    _L0_gnn_all = _L0_gnn_setup()
    _L0_gnn_in = {k: v for k, v in _L0_gnn_all.items() if k in ('Wk', 'Wq', 'Wv', 'Wa', 'rel_pri', 'rel_att', 'rel_msg', 'skip', 'ln_gamma', 'ln_beta')}
    del _L0_gnn_all

    def _L1_gnn_setup():
        import jax, jax.numpy as jnp
        import numpy as np
        EPS = 1e-05

        def gcn_conv(x, W, b, src, dst, ew, num_nodes):
            h = x @ W
            deg = jax.ops.segment_sum(ew, dst, num_segments=num_nodes)
            dinv = jnp.where(deg > 0, jax.lax.rsqrt(deg), 0.0)
            norm = dinv[src] * ew * dinv[dst]
            agg = jax.ops.segment_sum(h[src] * norm[:, None], dst, num_segments=num_nodes)
            return agg + b

        def batch_norm(x, gamma, beta):
            mu = jnp.mean(x, axis=0)
            var = jnp.mean((x - mu) ** 2, axis=0)
            return (x - mu) * jax.lax.rsqrt(var + EPS) * gamma + beta
        key = jax.random.key(seed)
        ks = jax.random.split(key, 16)
        N, E, D_IN, D_H = (12500, 200000, 128, 128)
        x = jax.random.normal(ks[0], (N, D_IN), dtype=jnp.float32)
        edge_index = jax.random.randint(ks[1], (2, E), 0, N, dtype=jnp.int64)
        edge_weight = jax.random.uniform(ks[2], (E,), dtype=jnp.float32)
        batch = jnp.zeros((N,), dtype=jnp.int64)
        s = 1.0 / np.sqrt(D_H)
        W1 = jax.random.uniform(ks[3], (D_IN, D_H), jnp.float32, -s, s)
        b1 = jnp.zeros((D_H,), jnp.float32)
        W2 = jax.random.uniform(ks[4], (D_H, D_H), jnp.float32, -s, s)
        b2 = jnp.zeros((D_H,), jnp.float32)
        W3 = jax.random.uniform(ks[5], (D_H, D_H), jnp.float32, -s, s)
        b3 = jnp.zeros((D_H,), jnp.float32)
        g1 = jnp.ones((D_H,), jnp.float32)
        be1 = jnp.zeros((D_H,), jnp.float32)
        g2 = jnp.ones((D_H,), jnp.float32)
        be2 = jnp.zeros((D_H,), jnp.float32)
        g3 = jnp.ones((D_H,), jnp.float32)
        be3 = jnp.zeros((D_H,), jnp.float32)
        return {'x': x, 'edge_index': edge_index, 'edge_weight': edge_weight, 'batch': batch, 'W1': W1, 'b1': b1, 'W2': W2, 'b2': b2, 'W3': W3, 'b3': b3, 'g1': g1, 'be1': be1, 'g2': g2, 'be2': be2, 'g3': g3, 'be3': be3}
    _L1_gnn_all = _L1_gnn_setup()
    _L1_gnn_in = {k: v for k, v in _L1_gnn_all.items() if k in ('W1', 'b1', 'W2', 'b2', 'W3', 'b3', 'g1', 'be1', 'g2', 'be2', 'g3', 'be3')}
    del _L1_gnn_all
    return {'x': x, 'src': src, 'dst': dst, 'edge_type_6': edge_type_6, 'edge_weight': edge_weight, 'node_type_4': node_type_4, 'L0_gnn_Wk': _L0_gnn_in['Wk'], 'L0_gnn_Wq': _L0_gnn_in['Wq'], 'L0_gnn_Wv': _L0_gnn_in['Wv'], 'L0_gnn_Wa': _L0_gnn_in['Wa'], 'L0_gnn_rel_pri': _L0_gnn_in['rel_pri'], 'L0_gnn_rel_att': _L0_gnn_in['rel_att'], 'L0_gnn_rel_msg': _L0_gnn_in['rel_msg'], 'L0_gnn_skip': _L0_gnn_in['skip'], 'L0_gnn_ln_gamma': _L0_gnn_in['ln_gamma'], 'L0_gnn_ln_beta': _L0_gnn_in['ln_beta'], 'L1_gnn_W1': _L1_gnn_in['W1'], 'L1_gnn_b1': _L1_gnn_in['b1'], 'L1_gnn_W2': _L1_gnn_in['W2'], 'L1_gnn_b2': _L1_gnn_in['b2'], 'L1_gnn_W3': _L1_gnn_in['W3'], 'L1_gnn_b3': _L1_gnn_in['b3'], 'L1_gnn_g1': _L1_gnn_in['g1'], 'L1_gnn_be1': _L1_gnn_in['be1'], 'L1_gnn_g2': _L1_gnn_in['g2'], 'L1_gnn_be2': _L1_gnn_in['be2'], 'L1_gnn_g3': _L1_gnn_in['g3'], 'L1_gnn_be3': _L1_gnn_in['be3']}

def reference(x, src, dst, edge_type_6, edge_weight, node_type_4, L0_gnn_Wk, L0_gnn_Wq, L0_gnn_Wv, L0_gnn_Wa, L0_gnn_rel_pri, L0_gnn_rel_att, L0_gnn_rel_msg, L0_gnn_skip, L0_gnn_ln_gamma, L0_gnn_ln_beta, L1_gnn_W1, L1_gnn_b1, L1_gnn_W2, L1_gnn_b2, L1_gnn_W3, L1_gnn_b3, L1_gnn_g1, L1_gnn_be1, L1_gnn_g2, L1_gnn_be2, L1_gnn_g3, L1_gnn_be3):
    import jax
    import jax.numpy as jnp

    def _L0_gnn_ref(x, src, dst, ntype, etype, Wk, Wq, Wv, Wa, rel_pri, rel_att, rel_msg, skip, ln_gamma, ln_beta):
        import jax, jax.numpy as jnp
        import numpy as np
        N, E, DIM, H, T, R = (6250, 50000, 128, 8, 4, 6)
        D = DIM // H

        def _typed_linear(x, W, types):
            out = jnp.zeros((x.shape[0], W.shape[-1]), x.dtype)
            for t in range(W.shape[0]):
                out = jnp.where((types == t)[:, None], x @ W[t], out)
            return out

        def _typed_rel(xe, W, etype):
            out = jnp.zeros_like(xe)
            for r in range(W.shape[1]):
                yr = jnp.einsum('ehd,hdo->eho', xe, W[:, r])
                out = jnp.where((etype == r)[:, None, None], yr, out)
            return out
        k = _typed_linear(x, Wk, ntype).reshape(N, H, D)
        q = _typed_linear(x, Wq, ntype).reshape(N, H, D)
        v = _typed_linear(x, Wv, ntype).reshape(N, H, D)
        k_e = k[src]
        q_e = q[dst]
        v_e = v[src]
        kw = _typed_rel(k_e, rel_att, etype)
        a = (kw * q_e).sum(-1) * rel_pri.T[etype] / jnp.sqrt(jnp.float32(D))
        m = _typed_rel(v_e, rel_msg, etype)
        amax = jax.lax.stop_gradient(jax.ops.segment_max(a, dst, num_segments=N))
        amax = jnp.where(jnp.isfinite(amax), amax, 0.0)
        ex = jnp.exp(a - amax[dst])
        den = jax.ops.segment_sum(ex, dst, num_segments=N)
        attn = ex / jnp.maximum(den[dst], 1e-09)
        h = jax.ops.segment_sum(m * attn[:, :, None], dst, num_segments=N).reshape(N, DIM)
        h = _typed_linear(h, Wa, ntype)
        gate = jax.nn.sigmoid(skip)[ntype][:, None]
        h = h * gate + x * (1.0 - gate)
        y = x + h
        mu = y.mean(-1, keepdims=True)
        var = ((y - mu) ** 2).mean(-1, keepdims=True)
        return (y - mu) / jnp.sqrt(var + 1e-05) * ln_gamma + ln_beta

    def _L1_gnn_ref(x, edge_index, edge_weight, batch, W1, b1, W2, b2, W3, b3, g1, be1, g2, be2, g3, be3):
        import jax, jax.numpy as jnp
        import numpy as np
        EPS = 1e-05

        def gcn_conv(x, W, b, src, dst, ew, num_nodes):
            h = x @ W
            deg = jax.ops.segment_sum(ew, dst, num_segments=num_nodes)
            dinv = jnp.where(deg > 0, jax.lax.rsqrt(deg), 0.0)
            norm = dinv[src] * ew * dinv[dst]
            agg = jax.ops.segment_sum(h[src] * norm[:, None], dst, num_segments=num_nodes)
            return agg + b

        def batch_norm(x, gamma, beta):
            mu = jnp.mean(x, axis=0)
            var = jnp.mean((x - mu) ** 2, axis=0)
            return (x - mu) * jax.lax.rsqrt(var + EPS) * gamma + beta
        N = x.shape[0]
        loop = jnp.arange(N, dtype=edge_index.dtype)
        src = jnp.concatenate([edge_index[0], loop])
        dst = jnp.concatenate([edge_index[1], loop])
        ew = jnp.concatenate([edge_weight, jnp.ones((N,), edge_weight.dtype)])
        h = gcn_conv(x, W1, b1, src, dst, ew, N)
        h = jax.nn.relu(batch_norm(h, g1, be1))
        h = gcn_conv(h, W2, b2, src, dst, ew, N)
        h = jax.nn.relu(batch_norm(h, g2, be2))
        h = gcn_conv(h, W3, b3, src, dst, ew, N)
        h = batch_norm(h, g3, be3)
        return h
    edge_index = jnp.stack([src, dst])
    batch0 = jnp.zeros((6250,), jnp.int32)
    x = _layernorm(x + _L0_gnn_ref(x, src, dst, node_type_4, edge_type_6, L0_gnn_Wk, L0_gnn_Wq, L0_gnn_Wv, L0_gnn_Wa, L0_gnn_rel_pri, L0_gnn_rel_att, L0_gnn_rel_msg, L0_gnn_skip, L0_gnn_ln_gamma, L0_gnn_ln_beta), axis=-1)
    x = _layernorm(x + _L1_gnn_ref(x, edge_index, edge_weight, batch0, L1_gnn_W1, L1_gnn_b1, L1_gnn_W2, L1_gnn_b2, L1_gnn_W3, L1_gnn_b3, L1_gnn_g1, L1_gnn_be1, L1_gnn_g2, L1_gnn_be2, L1_gnn_g3, L1_gnn_be3), axis=-1)
    return x

_drawn_inputs = setup_inputs


def setup_inputs(seed=0):
    import zlib

    import numpy as np

    out = dict(_drawn_inputs(seed))
    spreads = {'L0_gnn_skip': (1.0, 0.6),
     'L0_gnn_ln_gamma': (1.0, 0.2),
     'L0_gnn_ln_beta': (0.0, 0.1),
     'L1_gnn_b1': (0.0, 0.8),
     'L1_gnn_b2': (0.0, 0.8),
     'L1_gnn_b3': (0.0, 0.8),
     'L1_gnn_g1': (1.0, 0.2),
     'L1_gnn_be1': (0.0, 0.1),
     'L1_gnn_g2': (1.0, 0.2),
     'L1_gnn_be2': (0.0, 0.1),
     'L1_gnn_g3': (1.0, 0.2),
     'L1_gnn_be3': (0.0, 0.1)}
    factors = {}
    for name, (base, spread) in spreads.items():
        noise = np.random.default_rng([zlib.crc32(name.encode()), seed]).standard_normal(out[name].shape)
        drawn = base * np.exp(spread * noise) if base else spread * noise
        out[name] = jnp.asarray(drawn.astype(out[name].dtype))
    for name, factor in factors.items():
        out[name] = (out[name] * factor).astype(out[name].dtype)
    return out
```

```python
from contextlib import ExitStack

import concourse.bass as bass
from concourse import mybir

F32 = mybir.dt.float32
BF16 = mybir.dt.bfloat16
I32 = mybir.dt.int32
ALU = mybir.AluOpType
ACT = mybir.ActivationFunctionType
AX = mybir.AxisListType

P = 128
BIG = 1.0e30
PAD_DST = 20000
EPS = 1e-5
TPB = 16
GRP = 4
NG = TPB // GRP


def steps_by_pairs(eng, first, last, step, tail=0):
    for n in range(first, 2):
        step(n, n // 2, n % 2, True)
    with eng.Fori(1, (last - tail) // 2) as i:
        for par in (0, 1):
            step(2 * i + par, i, par, False)
    for n in range(2 * ((last - tail) // 2), last):
        step(n, n // 2, n % 2, False)


class Links:

    def __init__(self, eng, sem):
        self.eng, self.sem, self.n, self.base = eng, sem, 0, 0

    def at(self, base):
        self.base, self.n = base, 0

    def inc(self, ins):
        self.n += 1
        ins.then_inc(self.sem, 1)

    def wait(self, back=0):
        self.eng.wait_ge(self.sem, self.base + (self.n - back))

    def link(self, ins):
        self.inc(ins)
        self.wait()


def gnn(nc, x, src, dst, etype, ew, ntype, Wk, Wq, Wv, Wa, rel_pri, rel_att, rel_msg, skip, gamma, beta,
        W1, b1, W2, b2, W3, b3, g1, be1, g2, be2, g3, be3, out):
    N, D = x.shape
    E = src.shape[0]
    T = Wk.shape[0]
    H, R = rel_pri.shape
    DH = D // H
    assert D == P and TPB * H == P and D // DH == H
    NT = -(-N // P)
    NF = N // P
    NR = N - NF * P
    NP_ = NT * P
    NW = NP_ + P
    ET = -(-E // (P * TPB)) * TPB
    NB = ET // TPB
    EG = -(-ET // P)
    EFULL = (E // (P * P)) * P * P
    GF = EFULL // (P * P)
    TR = (E - EFULL) // P
    ER = E - EFULL - TR * P
    assert EG == GF + 1 and NR > 0 and ER > 0 and NT % 2 == 1 and NB % 2 == 0
    CH = [(c, min(512, NP_ - c)) for c in range(0, NP_, 512)]
    NCH = len(CH)

    kv_tab = nc.dram_tensor("kv_tab", (N * R, 2 * D), F32, kind="Internal").ap()
    q_tab = nc.dram_tensor("q_tab", (NW, D), F32, kind="Internal").ap()
    h_tab = [nc.dram_tensor(f"h_tab{i}", (N, D), F32, kind="Internal").ap() for i in range(3)]
    rel_d = nc.dram_tensor("rel_d", (EG * P * P,), BF16, kind="Internal").ap()
    negf_d = nc.dram_tensor("negf_d", (EG * P * H, P), F32, kind="Internal").ap()
    negb_d = nc.dram_tensor("negb_d", (EG * P * H, P), F32, kind="Internal").ap()

    with ExitStack() as ctx:
        def sb(name, shape, dt=F32):
            return ctx.enter_context(nc.sbuf_tensor(name, shape, dt))

        def sem(name):
            return ctx.enter_context(nc.semaphore(name))

        bank = [ctx.enter_context(nc.psum_tensor(f"bank{i}", [P, 512], F32)) for i in range(8)]

        xr = sb("xr", [P, NT, D])
        acc = sb("acc", [P, NW])
        hd = sb("hd", [P, NW])
        earr = sb("earr", [P, 4, EG * P])
        rel_c, idx_c, src_c, ew_c = (earr[:, k, :] for k in range(4))
        base_row = sb("base_row", [1, ET], I32)
        big = sb("big", [P, 2 * TPB * 2 * D])
        kv = big[:, :].rearrange("p (a t f) -> p a t f", a=2, t=TPB)
        relb = sb("relb", [P, 2, TPB * P], BF16)
        negs = sb("negs", [P, 2, 2, P])
        qwin = sb("qwin", [P, 2 * GRP, D])
        ohT = sb("ohT", [P, 2, GRP * P])
        oh = sb("oh", [P, NG, GRP, P])
        stage = sb("stage", [P, 2, R, 2 * D])
        gring = stage[:, :, :, :].rearrange("p a r f -> p (a r f)")[:, 0:TPB * D].rearrange("p (t f) -> p t f", t=TPB)
        bd = sb("bd", [P, 2, R, D])
        wkqv = sb("wkqv", [P, 3, T, D])
        wa = sb("wa", [P, T, D])
        wg = sb("wg", [P, 3, D])
        xm = sb("xm", [P, 2, T, D])
        xT = sb("xT", [P, 2, T, D])
        qkv = sb("qkv", [P, 2, 3, D])
        idxr = sb("idxr", [P, 2, TPB], I32)
        logit = sb("logit", [P, P])
        mxf = sb("mxf", [P, P])
        mxb = sb("mxb", [P, P])
        dif = sb("dif", [P, P])
        exT = sb("exT", [P, P])
        exw = sb("exw", [P, TPB, H + 1])
        rhs = sb("rhs", [P, 2, 2 * TPB])
        sx = sb("sx", [H, 2, TPB + 1])
        sr = sb("sr", [H, TPB + 1])
        negall = sb("negall", [H, 2, TPB])
        ini = sb("ini", [P, 4])
        tmp16 = sb("tmp16", [P, TPB])
        nodec = sb("nodec", [P, NT, H + 1])
        shf = sb("shf", [P, NT])
        fd = sb("fd", [H, 1])
        f9 = sb("f9", [H + 1, 1])
        iota_j = sb("iota_j", [P, P])
        iota_p = sb("iota_p", [P, 1])
        ident = sb("ident", [P, P])
        tsel = sb("tsel", [P, TPB])
        hselT = sb("hselT", [H, P])
        hsel = sb("hsel", [P, H])
        fsel = sb("fsel", [H + 1, P])
        dsel = sb("dsel", [H + 1, P])
        zrow = xm[:, 0, 0, :]
        pri = sb("pri", [P, R])
        nti = sb("nti", [NT, P], I32)
        ntf = sb("ntf", [NT, P])
        nt_c = sb("nt_c", [P, NT])
        tmask = sb("tmask", [P, NT, T])
        gmask = sb("gmask", [P, NT, T])
        keep = sb("keep", [P, NT])
        sk = sb("sk", [P, 3, T])
        lnw = sb("lnw", [P, 2, D])
        gcnv = sb("gcnv", [P, 9])
        bst = sb("bst", [P, NT, 6])
        mv = sb("mv", [P, NT, 2])
        rs = sb("rs", [P, NT])
        bn = sb("bn", [P, 4])
        epsc = sb("epsc", [P, 2])

        ei = big[:, 0:EG * 5 * P].bitcast(I32).rearrange("p (g k e) -> p g k e", g=EG, k=5)
        o = EG * 5 * P
        ewi = big[:, o:o + EG * P].rearrange("p (g e) -> p g e", g=EG)
        o += EG * P
        ef = big[:, o:o + 2 * 4 * P].rearrange("p (a k e) -> p a k e", a=2, k=4)
        o += 2 * 4 * P
        assert o <= big.shape[1]
        nb = ohT[:, :, :].rearrange("p a (k e) -> p a k e", k=4)
        ro = oh[:, :, :, :]
        relw = qwin[:, :, :].rearrange("p a f -> p (a f)").bitcast(BF16).rearrange("p (a e) -> p a e", a=16)

        pads_set = sem("pads_set")
        edges_in = sem("edges_in")
        weights_in = sem("weights_in")
        x_in = sem("x_in")
        const_link = sem("const_link")
        consts_ready = sem("consts_ready")
        edge_rows = sem("edge_rows")
        edge_turned = sem("edge_turned")
        edge_cols = sem("edge_cols")
        edge_saved = [sem(f"edge_saved{a}") for a in range(2)]
        dve_link = sem("dve_link")
        nt_ready, nt_turned, hsel_turned, masks_ready, hsel_ready = (
            sem(n) for n in ("nt_ready", "nt_turned", "hsel_turned", "masks_ready", "hsel_ready"))
        skip_exp = sem("skip_exp")
        xm_ready, x_turned, xT_ready, qkv_done, qkv_ready, tab_k, tab_v, tab_kv, k_copied, v_copied, kv_copied = (
            sem(n) for n in ("xm_ready", "x_turned", "xT_ready", "qkv_done", "qkv_ready", "tab_k", "tab_v",
                             "tab_kv", "k_copied", "v_copied", "kv_copied"))
        tab_saved = [sem(f"tab_saved{a}") for a in range(2)]
        q_saved = [sem(f"q_saved{a}") for a in range(2)]
        zeros_saved = sem("zeros_saved")
        tabs_complete = sem("tabs_complete")
        idx_ready = sem("idx_ready")
        gathers_begun = sem("gathers_begun")
        kv_land = [[sem(f"kv_land{a}_{g}") for g in range(NG)] for a in range(2)]
        batch_in = [sem(f"batch_in{a}") for a in range(2)]
        qwin_in = [sem(f"qwin_in{a}") for a in range(2)]
        ohT_ready, q_done, logit_done, logit_turned = (
            sem(n) for n in ("ohT_ready", "q_done", "logit_done", "logit_turned"))
        fwd_ends, fwd_chained, fwd_carry, fwd_spread = (
            sem(n) for n in ("fwd_ends", "fwd_chained", "fwd_carry", "fwd_spread"))
        bwd_ends, bwd_chained, bwd_carry, bwd_spread = (
            sem(n) for n in ("bwd_ends", "bwd_chained", "bwd_carry", "bwd_spread"))
        f_diff, f_ready, dif_ready, exT_ready, ex_turned, exw_ready = (
            sem(n) for n in ("f_diff", "f_ready", "dif_ready", "exT_ready", "ex_turned", "exw_ready"))
        vw_ready, oh_ready, agg_done, den_done, acc_added, den_added = (
            sem(n) for n in ("vw_ready", "oh_ready", "agg_done", "den_done", "acc_added", "den_added"))
        scaled, f_spread, ewcol_ready = (sem(n) for n in ("scaled", "f_spread", "ewcol_ready"))
        den_spread, attn_scaled, types_done, y_sum, y_normed, x1_ready, deg_ready, root_ready, dinv_ready = (
            sem(n) for n in ("den_spread", "attn_scaled", "types_done", "y_sum", "y_normed", "x1_ready",
                             "deg_ready", "root_ready", "dinv_ready"))
        var_ready, std_ready, stat_done, shift_ready, y_set, xb_ready, den_turned, den_wide = (
            sem(n) for n in ("var_ready", "std_ready", "stat_done", "shift_ready", "y_set", "xb_ready", "den_turned", "den_wide"))
        x1_turned, acc_set, rows_turned, rows_ready, tab_complete = (
            sem(n) for n in ("x1_turned", "acc_set", "rows_turned", "rows_ready", "tab_complete"))
        rows_saved = [sem(f"rows_saved{a}") for a in range(2)]
        src_ready = sem("src_ready")
        row_land = [sem(f"row_land{g}") for g in range(NG)]
        wt_ready, sum_done, win_added, lin_done, h_scaled, h_ready, bn_ready, act_ready, h_turned = (
            sem(n) for n in ("wt_ready", "sum_done", "win_added", "lin_done", "h_scaled", "h_ready", "bn_ready",
                             "act_ready", "h_turned"))
        res_added, out_ready, out_saved = (sem(n) for n in ("res_added", "out_ready", "out_saved"))

        loads = []
        per_group = lambda a: a.rearrange("(g p e) -> p g e", p=P, e=P)
        for k, a in ((0, dst), (3, src), (4, etype)):
            loads.append((ei[:, 0:GF, k, :], per_group(a[0:EFULL])))
            loads.append((ei[0:TR, GF, k, :], a[EFULL:EFULL + TR * P].rearrange("(p e) -> p e", e=P)))
            loads.append((ei[TR:TR + 1, GF, k, 0:ER], a[EFULL + TR * P:E].rearrange("(p e) -> p e", p=1)))
        loads.append((ewi[:, 0:GF, :], per_group(ew[0:EFULL])))
        loads.append((ewi[0:TR, GF, :], ew[EFULL:EFULL + TR * P].rearrange("(p e) -> p e", e=P)))
        loads.append((ewi[TR:TR + 1, GF, 0:ER], ew[EFULL + TR * P:E].rearrange("(p e) -> p e", p=1)))
        loads.append((ei[:, 1:GF, 1, :], per_group(dst[P * P - 1:EFULL - 1])))
        loads.append((ei[1:P, 0, 1, :], dst[P - 1:P * P - 1].rearrange("(p e) -> p e", e=P)))
        loads.append((ei[0:1, 0, 1, 1:P], dst[0:P - 1].rearrange("(p e) -> p e", p=1)))
        loads.append((ei[0:TR, GF, 1, :], dst[EFULL - 1:EFULL - 1 + TR * P].rearrange("(p e) -> p e", e=P)))
        loads.append((ei[TR:TR + 1, GF, 1, 0:ER + 1], dst[EFULL + TR * P - 1:E].rearrange("(p e) -> p e", p=1)))
        loads.append((ei[:, 0:GF, 2, :], per_group(dst[1:EFULL + 1])))
        loads.append((ei[0:TR, GF, 2, :], dst[EFULL + 1:EFULL + 1 + TR * P].rearrange("(p e) -> p e", e=P)))
        loads.append((ei[TR:TR + 1, GF, 2, 0:ER - 1], dst[EFULL + TR * P + 1:E].rearrange("(p e) -> p e", p=1)))
        NFULL = E // P
        loads.append((base_row[0:1, 0:NFULL], dst[0:NFULL * P].rearrange("(a t e) -> a t e", a=1, e=P)[:, :, 0]))
        loads.append((base_row[0:1, NFULL:NFULL + 1], dst[NFULL * P:NFULL * P + 1].rearrange("(a t) -> a t", a=1)))

        row = lambda v: v.rearrange("(a n) -> a n", a=1)
        wloads = [(nti[0:NF, :], ntype[0:NF * P].rearrange("(t p) -> t p", p=P)),
                  (nti[NF:NT, 0:NR], row(ntype[NF * P:N])),
                  (sk[:, 0, :], row(skip).to_broadcast([P, T])),
                  (lnw[:, 0, :], row(gamma).to_broadcast([P, D])),
                  (lnw[:, 1, :], row(beta).to_broadcast([P, D])),
                  (wa[:, :, :], Wa.rearrange("t i o -> i t o"))]
        for k, w in enumerate((Wq, Wk, Wv)):
            wloads.append((wkqv[:, k, :, :], w.rearrange("t i o -> i t o")))
        for k, w in enumerate((W1, W2, W3)):
            wloads.append((wg[:, k, :], w))
        for k, v in enumerate((b1, b2, b3, g1, g2, g3, be1, be2, be3)):
            wloads.append((gcnv[:, k:k + 1], v.rearrange("(p a) -> p a", a=1)))
        for h in range(H):
            rows = slice(h * DH, (h + 1) * DH)
            wloads.append((pri[rows, :], rel_pri[h:h + 1, :].to_broadcast([DH, R])))
            for k, w in enumerate((rel_att, rel_msg)):
                wloads.append((bd[rows, k, :, h * DH:(h + 1) * DH], w[h].rearrange("r i o -> i r o")))
        PADS = 11

        block = ctx.enter_context(nc.Block())

        @block.sync
        def _(sp):
            sp.wait_ge(pads_set, PADS)
            with nc.allow_non_contiguous_dma(reason="short columns"):
                for o_, i_ in loads:
                    sp.dma_start(o_, i_).then_inc(edges_in, 16)
                for o_, i_ in wloads:
                    sp.dma_start(o_, i_).then_inc(weights_in, 16)
            sp.dma_start(xr[:, 0:NF, :], x[0:NF * P, :].rearrange("(i p) f -> p i f", p=P)).then_inc(x_in, 16)
            sp.dma_start(xr[0:NR, NF, :], x[NF * P:N, :]).then_inc(x_in, 16)

            for g in range(EG):
                n = min(P, ET - g * P)
                sp.wait_ge(edge_rows, g + 1)
                sp.dma_start(rel_d[g * P * P:g * P * P + n * P].rearrange("(p e) -> p e", e=P),
                             relw[0:n, g % 2, :]).then_inc(edge_saved[g % 2], 16)
                for k, d in enumerate((negf_d, negb_d)):
                    sp.dma_start(d[g * P * H:(g * P + n) * H, :].rearrange("(p h) e -> p h e", h=H),
                                 nb[0:n, g % 2, k:k + 1, :].to_broadcast([n, H, P])).then_inc(edge_saved[g % 2], 16)

            def save(n, i, par, peeled):
                rows = NR if (isinstance(n, int) and n == NF) else P
                sp.wait_ge(k_copied, n + 1)
                sp.wait_ge(v_copied, n + 1)
                sp.wait_ge(kv_copied, n + 1)
                tab = kv_tab.rearrange("(n r) f -> n (r f)", r=R)
                sp.dma_start(tab[bass.ds(n * P, rows), :],
                             stage[0:rows, par, :, :].rearrange("p r f -> p (r f)")).then_inc(tab_saved[par], 16)
                sp.dma_start(q_tab[bass.ds(n * P, P), :], qkv[:, par, 0, :]).then_inc(q_saved[par], 16)
            steps_by_pairs(sp, 0, NT, save)
            sp.wait_ge(masks_ready, 2)
            sp.dma_start(q_tab[NP_:NW, :], oh[:, 0, 0, :]).then_inc(zeros_saved, 16)
            for a in range(2):
                cnt = (NT + 1 - a) // 2
                sp.wait_ge(tab_saved[a], 16 * cnt)
                sp.wait_ge(q_saved[a], 16 * cnt)
            sp.wait_ge(zeros_saved, 16)
            for a in range(2):
                sp.wait_ge(edge_saved[a], 48 * ((EG + 1 - a) // 2))
            sp.sem_inc(tabs_complete, 1)

            def feed(b, i, par, peeled):
                if not peeled:
                    sp.wait_ge(ohT_ready, NG * (b - 1))
                    sp.wait_ge(dif_ready, b - 1)
                sp.dma_start(relb[:, par, :], rel_d[bass.ds(b * (TPB * P), TPB * P)].rearrange("(a n) -> a n", a=1)
                             .to_broadcast([P, TPB * P])).then_inc(batch_in[par], 16)
                sp.dma_start(negs[:, par, 0, :], negf_d[bass.ds(b * P, P), :]).then_inc(batch_in[par], 16)
                sp.dma_start(negs[:, par, 1, :], negb_d[bass.ds(b * P, P), :]).then_inc(batch_in[par], 16)
                for g in range(NG):
                    if not (isinstance(b, int) and NG * b + g < 2):
                        sp.wait_ge(q_done, NG * b + g - 1)
                    for s in range(GRP):
                        first = sp.value_load(base_row[0:1, bass.ds(b * TPB + (g * GRP + s), 1)], min_val=0, max_val=N - 1)
                        sp.dma_start(qwin[:, (g % 2) * GRP + s, :], q_tab[bass.ds(first, P), :])\
                          .then_inc(qwin_in[g % 2], 16)
            steps_by_pairs(sp, 0, NB, feed)

            for l in range(3):
                for c, (c0, cw) in enumerate(CH):
                    sp.wait_ge(rows_ready, NCH * l + c + 1)
                    rows, tiles = min(cw, N - c0), cw // P
                    a = (NCH * l + c) % 2
                    if rows == cw:
                        sp.dma_start(h_tab[l][c0:c0 + rows, :].rearrange("(i p) f -> p i f", p=P),
                                     xT[:, a, 0:tiles, :]).then_inc(rows_saved[a], 16)
                    else:
                        assert tiles == 1
                        sp.dma_start(h_tab[l][c0:N, :], xT[0:rows, a, 0, :]).then_inc(rows_saved[a], 16)
                for a in range(2):
                    sp.wait_ge(rows_saved[a], 16 * ((NCH * (l + 1) + 1 - a) // 2))
                sp.sem_inc(tab_complete, 1)
            for c, (c0, cw) in enumerate(CH):
                sp.wait_ge(out_ready, c0 // P + cw // P)
                if c0 + cw <= N:
                    sp.dma_start(out[c0:c0 + cw, :].rearrange("(i p) f -> p i f", p=P),
                                 xr[:, c0 // P:(c0 + cw) // P, :]).then_inc(out_saved, 16)
                else:
                    sp.dma_start(out[c0:N, :], xr[0:N - c0, c0 // P, :]).then_inc(out_saved, 16)
            sp.wait_ge(out_saved, 16 * NCH)

        @block.gpsimd
        def _(pool):
            G = nc.gpsimd
            link = Links(pool, const_link)
            G.iota(iota_j[:], [[1, P]], base=0, channel_multiplier=0, allow_small_or_imprecise_dtypes=True).then_inc(consts_ready, 1)
            G.iota(iota_p[:], [[1, 1]], base=0, channel_multiplier=1, allow_small_or_imprecise_dtypes=True).then_inc(consts_ready, 1)
            for t_, v_ in ((ident, 0.0), (hselT, 0.0), (fsel, 0.0), (dsel, 0.0), (tsel, 1.0)):
                link.inc(G.memset(t_[:, :], v_))
            link.wait()
            G.affine_select(out=ident[:, :], in_=ident[:, :], compare_op=ALU.not_equal, fill=1.0, base=0,
                            pattern=[[-1, P]], channel_multiplier=1).then_inc(consts_ready, 1)
            v_ = hselT[:, :].rearrange("h (t g) -> h t g", g=H)
            G.affine_select(out=v_, in_=v_, compare_op=ALU.not_equal, fill=1.0, base=0,
                            pattern=[[0, TPB], [1, H]], channel_multiplier=-1).then_inc(consts_ready, 1)
            v_ = fsel[:, :].rearrange("h (g d) -> h g d", d=DH)
            G.affine_select(out=v_, in_=v_, compare_op=ALU.not_equal, fill=1.0, base=0,
                            pattern=[[1, H], [0, DH]], channel_multiplier=-1).then_inc(consts_ready, 1)
            G.affine_select(out=dsel[:, :], in_=dsel[:, :], compare_op=ALU.not_equal, fill=1.0, base=-H,
                            pattern=[[0, P]], channel_multiplier=1).then_inc(consts_ready, 1)
            link.link(G.affine_select(out=tsel[:, :], in_=tsel[:, :], compare_op=ALU.is_ge, fill=0.0, base=0,
                                      pattern=[[-H, TPB]], channel_multiplier=1))
            G.affine_select(out=tsel[:, :], in_=tsel[:, :], compare_op=ALU.is_ge, fill=0.0, base=H - 1,
                            pattern=[[H, TPB]], channel_multiplier=-1).then_inc(consts_ready, 1)

            pool.wait_ge(tabs_complete, 1)

            def gather(b, i, par, peeled):
                pool.wait_ge(idx_ready, b + 1)
                pool.sem_inc(gathers_begun, 1)
                for g in range(NG):
                    if not peeled:
                        pool.wait_ge(agg_done, NG * (b - 2) + g + 1)
                        pool.sem_inc(gathers_begun, 1)
                    for s in range(GRP):
                        t = g * GRP + s
                        G.indirect_dma_start(kv[:, par, t, :], None, kv_tab,
                                             bass.IndirectOffsetOnAxis(idxr[:, par, t:t + 1], 0))\
                         .then_inc(kv_land[par][g], 16)
            steps_by_pairs(pool, 0, NB, gather)

            pool.wait_ge(y_set, 1)
            G.tensor_tensor(xr[:, :, :], xr[:, :, :], lnw[:, 1:2, :].to_broadcast([P, NT, D]), ALU.add).then_inc(xb_ready, 1)
            for l in range(3):
                pool.wait_ge(tab_complete, l + 1)

                def gather_h(b, i, par, peeled):
                    B = b + NB * l
                    pool.wait_ge(src_ready, B + 1)
                    pool.sem_inc(gathers_begun, 1)
                    for g in range(NG):
                        if not (isinstance(B, int) and B == 0):
                            pool.wait_ge(sum_done, NG * (B - 1) + g + 1)
                            pool.sem_inc(gathers_begun, 1)
                        for s in range(GRP):
                            t = g * GRP + s
                            G.indirect_dma_start(gring[:, t, :], None, h_tab[l],
                                                 bass.IndirectOffsetOnAxis(idxr[:, par, t:t + 1], 0))\
                             .then_inc(row_land[g], 16)
                steps_by_pairs(pool, 0, NB, gather_h)

        @block.scalar
        def _(act):
            S = nc.scalar
            for g in range(EG):
                n = min(P, ET - g * P)
                act.wait_ge(edge_turned, g + 1)
                S.activation(earr[:, :, g * P:g * P + n],
                             bank[g % 2][:, :].rearrange("p (k t) -> p k t", k=4)[:, :, 0:n], ACT.Copy)\
                 .then_inc(edge_cols, 1)
            act.wait_ge(weights_in, 16 * len(wloads))
            S.activation(sk[:, 1, :], sk[:, 0, :], ACT.Exp, scale=-1.0).then_inc(skip_exp, 1)

            def copy_xT(n, par):
                act.wait_ge(x_turned, n + 1)
                if not isinstance(n, int) or n >= 2:
                    act.wait_ge(qkv_done, n - 1)
                S.activation(xT[:, par, :, :], bank[par][:, :].rearrange("p (t f) -> p t f", t=T), ACT.Copy)\
                 .then_inc(xT_ready, 1)

            def copy_qkv(n, i, par):
                act.wait_ge(qkv_done, n + 1)
                if not isinstance(n, int) or n >= 2:
                    act.wait_ge(tab_kv, n - 1)
                    act.wait_ge(q_saved[par], 16 * i)
                S.activation(qkv[:, par, :, :], bank[2 + par][:, 0:3 * D].rearrange("p (k f) -> p k f", k=3), ACT.Copy)\
                 .then_inc(qkv_ready, 1)

            def copy_tab(n, i, par):
                act.wait_ge(tab_kv, n + 1)
                if not isinstance(n, int) or n >= 2:
                    act.wait_ge(tab_saved[par], 16 * i)
                S.activation(stage[:, par, GRP:R, :].rearrange("p r (k f) -> p k r f", k=2),
                             bank[6][:, :].rearrange("p (k r f) -> p k r f", k=2, r=R - GRP), ACT.Copy)\
                 .then_inc(kv_copied, 1)

            act.wait_ge(edge_cols, EG)
            copy_xT(0, 0)
            copy_xT(1, 1)
            copy_qkv(0, 0, 0)

            def table(n, i, par, peeled):
                copy_xT(n + 2, par)
                copy_qkv(n + 1, i + (par == 1), 1 - par)
                copy_tab(n, i, par)
            steps_by_pairs(act, 0, NT - 3, table)
            table(NT - 3, (NT - 3) // 2, (NT - 3) % 2, False)
            copy_qkv(NT - 1, (NT - 1) // 2, (NT - 1) % 2)
            copy_tab(NT - 2, (NT - 2) // 2, (NT - 2) % 2)
            copy_tab(NT - 1, (NT - 1) // 2, (NT - 1) % 2)

            def indices(b, par, peeled, n_land):
                if not peeled:
                    for g in range(NG):
                        act.wait_ge(kv_land[par][g], n_land)
                S.activation(idxr[:, par, :], idx_c[:, bass.ds(b * TPB, TPB)], ACT.Copy).then_inc(idx_ready, 1)

            def weights(c):
                if not (isinstance(c, int) and c == 0):
                    act.wait_ge(agg_done, NG * c)
                    act.wait_ge(den_done, NG * c)
                act.wait_ge(edge_cols, EG)
                S.activation(exw[:, :, H], ew_c[:, bass.ds(c * TPB, TPB)], ACT.Copy).then_inc(ewcol_ready, 1)
                act.wait_ge(f_diff, c + 1)
                if not (isinstance(c, int) and c == 0):
                    act.wait_ge(scaled, 2 * c)
                S.activation(f9[0:H, :], fd[:, :], ACT.Exp).then_inc(f_ready, 1)
                act.wait_ge(dif_ready, c + 1)
                if not (isinstance(c, int) and c == 0):
                    act.wait_ge(ex_turned, c)
                S.activation(exT[:, :], dif[:, :], ACT.Exp).then_inc(exT_ready, 1)
                act.wait_ge(ex_turned, c + 1)
                S.activation(exw[:, :, 0:H], bank[2][:, P:2 * P].rearrange("p (t h) -> p t h", h=H), ACT.Copy)\
                 .then_inc(exw_ready, 1)

            act.wait_ge(consts_ready, 7)
            indices(0, 0, True, 0)

            def attend(b, i, par, peeled):
                if isinstance(b, int) and b == 0:
                    indices(1, 1, True, 0)
                    return
                indices(b + 1, 1 - par, False, 64 * (i + par))
                weights(b - 1)
            attend(0, 0, 0, True)
            attend(1, 0, 1, True)
            with act.Fori(1, NB // 2 - 1) as i:
                for par in (0, 1):
                    attend(2 * i + par, i, par, False)
            attend(NB - 2, NB // 2 - 1, 0, False)
            weights(NB - 2)
            weights(NB - 1)

            def root(n, w):
                act.wait_ge(var_ready, n)
                S.activation(rs[:, 0:w], mv[:, 0:w, 1], ACT.Sqrt, bias=epsc[:, 0:1]).then_inc(std_ready, 1)

            act.wait_ge(deg_ready, 1)
            S.activation(nodec[:, :, H], nodec[:, :, H], ACT.Sqrt).then_inc(root_ready, 1)
            act.wait_ge(deg_ready, 3)
            S.activation(big[:, 0:NP_].rearrange("p (n h d) -> p n h d", h=H, d=DH),
                         nodec[:, :, 0:H].rearrange("p n (h a) -> p n h a", a=1).to_broadcast([P, NT, H, DH]), ACT.Copy)\
             .then_inc(den_wide, 1)
            root(1, NT)

            def normalize(k):
                act.wait_ge(shift_ready, k)
                for n in range(NT):
                    if k == 2:
                        o_ = xr[:, n, :]
                    else:
                        o_ = big[:, n * D:(n + 1) * D]
                    S.activation(o_, big[:, n * D:(n + 1) * D], ACT.Identity, bias=shf[:, n:n + 1], scale=rs[:, n:n + 1])\
                     .then_inc(y_normed if k == 1 else x1_ready, 1)
            normalize(1)
            root(2, NT)
            normalize(2)
            def rows_out(l, c):
                c0, cw = CH[c]
                n, a, tiles = NCH * l + c, (NCH * l + c) % 2, cw // P
                act.wait_ge(rows_turned, n + 1)
                if n >= 2:
                    act.wait_ge(rows_saved[a], 16 * (n // 2))
                S.activation(xT[:, a, 0:tiles, :], bank[4 + n % 2][:, 0:cw].rearrange("p (t f) -> p t f", f=D),
                             ACT.Copy).then_inc(rows_ready, 1)

            for c in range(NCH):
                rows_out(0, c)
            for l in range(3):

                def sources(b, i, par, peeled):
                    B = b + NB * l
                    if not (isinstance(B, int) and B < 2):
                        for g in range(NG):
                            act.wait_ge(row_land[g], 64 * (B - 1))
                    S.activation(idxr[:, par, :], src_c[:, bass.ds(b * TPB, TPB)], ACT.Copy).then_inc(src_ready, 1)
                if l == 0:
                    for a in range(2):
                        for g in range(NG):
                            act.wait_ge(kv_land[a][g], 64 * (NB // 2))
                steps_by_pairs(act, 0, NB, sources)
                for c, (c0, cw) in enumerate(CH):
                    act.wait_ge(h_scaled, NCH * l + c + 1)
                    S.activation(hd[:, c0:c0 + cw], hd[:, c0:c0 + cw], ACT.Identity, bias=gcnv[:, l:l + 1])\
                     .then_inc(h_ready, 1)
                root(3 + l, 1)
                act.wait_ge(bn_ready, l + 1)
                for c, (c0, cw) in enumerate(CH):
                    S.activation(hd[:, c0:c0 + cw], hd[:, c0:c0 + cw], ACT.Relu if l < 2 else ACT.Identity,
                                 bias=bn[:, 1:2], scale=bn[:, 0:1]).then_inc(act_ready, 1)
                    if l < 2 and c >= 2:
                        rows_out(l + 1, c - 2)
                if l < 2:
                    rows_out(l + 1, NCH - 2)
                    rows_out(l + 1, NCH - 1)
            root(6, NT)

        @block.tensor
        def _(pe):
            M = nc.tensor
            pe.wait_ge(consts_ready, 7)
            for g in range(EG):
                n = min(P, ET - g * P)
                pe.wait_ge(edge_rows, g + 1)
                if g >= 2:
                    pe.wait_ge(edge_cols, g - 1)
                for k, a in enumerate((ro[0:n, g % 2, 0, :], ro[0:n, g % 2, 1, :], ef[0:n, g % 2, 3, :], ewi[0:n, g, :])):
                    last = M.transpose(bank[g % 2][:, k * P:k * P + n], a, ident[0:n, 0:n])
                last.then_inc(edge_turned, 1)
            M.transpose(bank[2][:, 0:H], hselT[:, :], ident[0:H, 0:H]).then_inc(hsel_turned, 1)
            pe.wait_ge(nt_ready, 1)
            M.transpose(bank[3][:, 0:NT], ntf[:, :], ident[0:NT, 0:NT]).then_inc(nt_turned, 1)
            pe.wait_ge(weights_in, 16 * len(wloads))
            pe.wait_ge(edge_cols, EG)
            pe.wait_ge(masks_ready, 1)
            pe.wait_ge(hsel_ready, 1)

            def turn(n, par):
                pe.wait_ge(xm_ready, n + 1)
                if not isinstance(n, int) or n >= 2:
                    pe.wait_ge(xT_ready, n - 1)
                for t in range(T):
                    last = M.transpose(bank[par][:, t * D:(t + 1) * D], xm[:, par, t, :], ident[:, :])
                last.then_inc(x_turned, 1)

            def project(n, par):
                pe.wait_ge(xT_ready, n + 1)
                if not isinstance(n, int) or n >= 2:
                    pe.wait_ge(qkv_ready, n - 1)
                o_ = bank[2 + par]
                for t in range(T):
                    M.matmul(o_[:, 0:D], xT[:, par, t, :], wkqv[:, 0, t, :], start=t == 0, stop=t == T - 1)
                for k in (1, 2):
                    for t in range(T):
                        last = M.matmul(o_[:, k * D:(k + 1) * D], wkqv[:, k, t, :], xT[:, par, t, :],
                                        start=t == 0, stop=t == T - 1)
                last.then_inc(qkv_done, 1)

            def relate(n, par):
                pe.wait_ge(qkv_ready, n + 1)
                first = isinstance(n, int) and n == 0
                for k, (o_, done, copied) in enumerate(((bank[4], tab_k, k_copied), (bank[5], tab_v, v_copied))):
                    if not first:
                        pe.wait_ge(copied, n)
                    M.matmul(o_[:, :], qkv[:, par, 1 + k, :], bd[:, k, 0:GRP, :].rearrange("p r f -> p (r f)"),
                             start=True, stop=True).then_inc(done, 1)
                if not first:
                    pe.wait_ge(kv_copied, n)
                w = (R - GRP) * D
                for k in range(2):
                    last = M.matmul(bank[6][:, k * w:(k + 1) * w], qkv[:, par, 1 + k, :],
                                    bd[:, k, GRP:R, :].rearrange("p r f -> p (r f)"), start=True, stop=True)
                last.then_inc(tab_kv, 1)

            turn(0, 0)
            turn(1, 1)
            project(0, 0)

            def table(n, i, par, peeled):
                turn(n + 2, par)
                project(n + 1, 1 - par)
                relate(n, par)
            steps_by_pairs(pe, 0, NT - 3, table)
            table(NT - 3, 0, (NT - 3) % 2, False)
            project(NT - 1, (NT - 1) % 2)
            relate(NT - 2, (NT - 2) % 2)
            relate(NT - 1, (NT - 1) % 2)
            pe.wait_ge(k_copied, NT)
            pe.wait_ge(v_copied, NT)
            pe.wait_ge(kv_copied, NT)
            pe.wait_ge(qkv_ready, NT)

            def q_rows(b, i, g):
                pe.wait_ge(ohT_ready, NG * b + g + 1)
                pe.wait_ge(qwin_in[g % 2], 64 * (NG // 2) * b + 64 * (g // 2 + 1))
                if not (isinstance(b, int) and NG * b + g < 2):
                    pe.wait_ge(logit_done, NG * b + g - 1)
                for s in range(GRP):
                    last = M.matmul(bank[g % 2][:, s * D:(s + 1) * D], ohT[:, g % 2, s * P:(s + 1) * P],
                                    qwin[:, (g % 2) * GRP + s, :], start=True, stop=True)
                last.then_inc(q_done, 1)

            def aggregate(c, g):
                pe.wait_ge(vw_ready, NG * c + g + 1)
                pe.wait_ge(oh_ready, NG * c + g + 1)
                first = isinstance(c, int) and NG * c + g < 2
                if not first:
                    pe.wait_ge(acc_added, TPB * c + GRP * (g - 1))
                par = None
                for s in range(GRP):
                    last = M.matmul(bank[4 + g % 2][:, s * P:(s + 1) * P], vw_of[0][:, g * GRP + s, D:2 * D],
                                    oh[:, g % 2, s, :], start=True, stop=True)
                last.then_inc(agg_done, 1)
                if not first:
                    pe.wait_ge(den_added, TPB * c + GRP * (g - 1))
                pe.wait_ge(exw_ready, c + 1)
                pe.wait_ge(ewcol_ready, c + 1)
                for s in range(GRP):
                    last = M.matmul(bank[6 + g % 2][0:H + 1, s * P:(s + 1) * P], exw[:, g * GRP + s, :],
                                    oh[:, g % 2, s, :], start=True, stop=True)
                last.then_inc(den_done, 1)

            vw_of = [None]

            def chain_f(c):
                pe.wait_ge(fwd_ends, c + 1)
                M.matmul(bank[3][0:H, 0:2 * TPB], hsel[:, :], rhs[:, 0, :], start=True, stop=True).then_inc(fwd_chained, 1)

            def spread_f(c, par_c):
                pe.wait_ge(fwd_carry, c + 1)
                M.matmul(bank[3][:, 64:64 + TPB], hselT[:, :], sx[:, par_c, 0:TPB], start=True, stop=True).then_inc(fwd_spread, 1)

            def chain_b(c):
                pe.wait_ge(bwd_ends, c + 1)
                M.matmul(bank[3][0:H, 128:128 + 2 * TPB], hsel[:, :], rhs[:, 1, :], start=True, stop=True).then_inc(bwd_chained, 1)

            def spread_b(c):
                pe.wait_ge(bwd_carry, c + 1)
                M.matmul(bank[3][:, 192:192 + TPB], hselT[:, :], sr[:, 1:TPB + 1], start=True, stop=True).then_inc(bwd_spread, 1)

            def turn_ex(c):
                pe.wait_ge(exT_ready, c + 1)
                pe.wait_ge(f_ready, c + 1)
                if not (isinstance(c, int) and c == 0):
                    pe.wait_ge(exw_ready, c)
                M.matmul(bank[2][:, 2 * P:2 * P + 1], fsel[0:H, :], f9[0:H, :], start=True, stop=True).then_inc(f_spread, 1)
                M.transpose(bank[2][:, P:2 * P], exT[:, :], ident[:, :]).then_inc(ex_turned, 1)

            def turn_logit(b):
                pe.wait_ge(logit_done, NG * (b + 1))
                if not (isinstance(b, int) and b == 0):
                    pe.wait_ge(dif_ready, b)
                M.transpose(bank[2][:, 0:P], logit[:, :], ident[:, :]).then_inc(logit_turned, 1)

            def attend(b, i, par, peeled):
                c = b - 1
                vw_of[0] = kv[:, 1 - par, :, :]
                if isinstance(b, int) and b == 0:
                    for g in range(NG):
                        q_rows(b, i, g)
                    turn_logit(b)
                    return
                q_rows(b, i, 0)
                chain_f(c)
                q_rows(b, i, 1)
                spread_f(c, 1 - par)
                chain_b(c)
                q_rows(b, i, 2)
                spread_b(c)
                turn_ex(c)
                aggregate(c, 0)
                aggregate(c, 1)
                q_rows(b, i, 3)
                aggregate(c, 2)
                aggregate(c, 3)
                turn_logit(b)
            steps_by_pairs(pe, 0, NB, attend)
            c = NB - 1
            vw_of[0] = kv[:, 1, :, :]
            chain_f(c)
            spread_f(c, 1)
            chain_b(c)
            spread_b(c)
            turn_ex(c)
            for g in range(NG):
                aggregate(c, g)

            pe.wait_ge(den_added, ET)
            pe.wait_ge(acc_added, ET)
            for n in range(NT):
                last = M.transpose(bank[0][:, n * (H + 1):(n + 1) * (H + 1)], hd[0:H + 1, n * P:(n + 1) * P],
                                   ident[0:H + 1, 0:H + 1])
            last.then_inc(den_turned, 1)
            pe.wait_ge(den_wide, 1)
            for c, (c0, cw) in enumerate(CH):
                if c >= 3:
                    pe.wait_ge(attn_scaled, c - 2)
                for t in range(cw // P):
                    last = M.transpose(bank[1 + c % 3][:, t * P:(t + 1) * P],
                                       big[:, c0 + t * P:c0 + (t + 1) * P],
                                       ident[:, :])
                last.then_inc(den_spread, 1)
            for n in range(NT):
                pe.wait_ge(attn_scaled, NCH)
                if n >= 2:
                    pe.wait_ge(y_sum, 8 * (n // 2 - 1) + 6 + n % 2 + 1)
                M.matmul(bank[4 + n % 2][:, :], acc[:, n * P:(n + 1) * P], wa[:, :, :].rearrange("p t f -> p (t f)"),
                         start=True, stop=True).then_inc(types_done, 1)
            pe.wait_ge(x1_ready, NT)
            for c, (c0, cw) in enumerate(CH):
                if c >= 2:
                    pe.wait_ge(acc_set, c - 1)
                for t in range(cw // P):
                    M.transpose(bank[c % 2][:, t * P:(t + 1) * P],
                                nodec[:, c0 // P + t, H:H + 1].to_broadcast([P, P]), ident[:, :])
                for t in range(cw // P):
                    last = M.transpose(bank[2 + c % 2][:, t * P:(t + 1) * P], xr[:, c0 // P + t, :], ident[:, :])
                last.then_inc(x1_turned, 1)
            for l in range(3):
                for c, (c0, cw) in enumerate(CH):
                    n = NCH * l + c
                    pe.wait_ge(acc_set, n + 1)
                    if n >= 2:
                        pe.wait_ge(rows_ready, n - 1)
                    for t in range(cw // P):
                        last = M.transpose(bank[4 + n % 2][:, t * P:(t + 1) * P], acc[:, c0 + t * P:c0 + (t + 1) * P],
                                           ident[:, :])
                    last.then_inc(rows_turned, 1)

                def sums(b, i, par, peeled):
                    B = b + NB * l
                    for g in range(NG):
                        pe.wait_ge(row_land[g], 64 * (B + 1))
                        pe.wait_ge(wt_ready, TPB * B + GRP * (g + 1))
                        if not (isinstance(B, int) and B == 0):
                            pe.wait_ge(win_added, TPB * (B - 1) + GRP * (g + 1))
                        for s in range(GRP):
                            last = M.matmul(bank[g][:, s * P:(s + 1) * P], gring[:, g * GRP + s, :], oh[:, g, s, :],
                                            start=True, stop=True)
                        last.then_inc(sum_done, 1)
                steps_by_pairs(pe, 0, NB, sums)
                pe.wait_ge(win_added, ET * (l + 1))
                for c, (c0, cw) in enumerate(CH):
                    if c >= 4:
                        pe.wait_ge(h_scaled, NCH * l + c - 3)
                    M.matmul(bank[c % 4][:, 0:cw], wg[:, l, :], acc[:, c0:c0 + cw], start=True, stop=True)\
                     .then_inc(lin_done, 1)
            for c, (c0, cw) in enumerate(CH):
                pe.wait_ge(act_ready, NCH * 2 + c + 1)
                if c >= 4:
                    pe.wait_ge(res_added, c - 3)
                for t in range(cw // P):
                    last = M.transpose(bank[4 + c % 4][:, t * P:(t + 1) * P], hd[:, c0 + t * P:c0 + (t + 1) * P],
                                       ident[:, :])
                last.then_inc(h_turned, 1)

        @block.vector
        def _(dve):
            V = nc.vector
            dl = Links(dve, dve_link)

            def load_starts(t):
                return nc.values_load_multi_w_load_instructions(
                    base_row[0:1, bass.ds(t, GRP)], engines=[mybir.EngineType.DVE], min_val=0, max_val=N - 1)[1]

            V.memset(ei[:, GF, 0:3, :], PAD_DST).then_inc(pads_set, 1)
            V.memset(ei[:, GF, 3:5, :], 0).then_inc(pads_set, 1)
            V.memset(ei[0:1, 0, 1, 0:1], -5).then_inc(pads_set, 1)
            V.memset(ewi[:, GF, :], 0.0).then_inc(pads_set, 1)
            V.memset(nti[:, :], 0).then_inc(pads_set, 1)
            V.memset(base_row[:, :], 0).then_inc(pads_set, 1)
            V.memset(bd[:, :, :, :], 0.0).then_inc(pads_set, 1)
            V.memset(xr[:, NF, :], 0.0).then_inc(pads_set, 1)
            V.memset(epsc[:, 0:1], EPS).then_inc(pads_set, 1)
            V.memset(epsc[:, 1:2], 1.0).then_inc(pads_set, 1)
            V.memset(f9[:, :], 1.0).then_inc(pads_set, 1)

            dve.wait_ge(edges_in, 16 * len(loads))
            for g in range(EG):
                n, a = min(P, ET - g * P), g % 2
                if g >= 2:
                    dve.wait_ge(edge_turned, g - 1)
                    dve.wait_ge(edge_saved[a], 48 * (g // 2))
                e_ = ef[0:n, a, :, :]
                dl.inc(V.tensor_copy(e_[:, 0:4, :], ei[0:n, g, 0:4, :]))
                dl.link(V.tensor_copy(ro[0:n, a, 2, :], ei[0:n, g, 4, :]))
                dl.inc(V.tensor_tensor(nb[0:n, a, 0, :], e_[:, 0, :], e_[:, 1, :], ALU.is_equal))
                dl.inc(V.tensor_tensor(nb[0:n, a, 1, :], e_[:, 0, :], e_[:, 2, :], ALU.is_equal))
                dl.inc(V.tensor_scalar(ro[0:n, a, 3, 0:1], e_[:, 0, 0:1], float(PAD_DST) - 1.0, e_[:, 0, 0:1],
                                       ALU.is_lt, ALU.mult))
                dl.link(V.scalar_tensor_tensor(out=ro[0:n, a, 1, :], in0=e_[:, 3, :], scalar=float(R),
                                               in1=ro[0:n, a, 2, :], op0=ALU.mult, op1=ALU.add))
                dl.inc(V.tensor_scalar(nb[0:n, a, 0:2, :], nb[0:n, a, 0:2, :], 1.0, BIG, ALU.subtract, ALU.mult))
                dl.inc(V.tensor_scalar(relw[0:n, a, :], e_[:, 0, :], ro[0:n, a, 3, 0:1], None, ALU.subtract))
                dl.wait(1)
                V.tensor_scalar(ro[0:n, a, 0, :], e_[:, 0, :], ro[0:n, a, 3, 0:1], None, ALU.subtract).then_inc(edge_rows, 1)
                dl.wait()
            dve.wait_ge(weights_in, 16 * len(wloads))
            V.tensor_copy(ntf[:, :], nti[:, :]).then_inc(nt_ready, 1)
            dve.wait_ge(skip_exp, 1)
            dl.link(V.tensor_scalar(sk[:, 1, :], sk[:, 1, :], 1.0, None, ALU.add))
            dl.link(V.reciprocal(sk[:, 2, :], sk[:, 1, :]))
            dl.link(V.tensor_scalar(pri[:, :], pri[:, :], float(DH) ** -0.5, None, ALU.mult))
            for r in range(R):
                dl.inc(V.tensor_scalar(bd[:, 0, r, :], bd[:, 0, r, :], pri[:, r:r + 1], None, ALU.mult))
            dve.wait_ge(hsel_turned, 1)
            V.tensor_copy(hsel[:, :], bank[2][:, 0:H]).then_inc(hsel_ready, 1)
            dve.wait_ge(nt_turned, 1)
            dl.link(V.tensor_copy(nt_c[:, :], bank[3][:, 0:NT]))
            for t in range(T):
                dl.inc(V.tensor_scalar(tmask[:, :, t], nt_c[:, :], float(t), None, ALU.is_equal))
            dl.wait()
            dl.link(V.tensor_tensor(gmask[:, :, :], tmask[:, :, :], sk[:, 2:3, :].to_broadcast([P, NT, T]), ALU.mult))
            dl.link(V.tensor_reduce(keep[:, :], gmask[:, :, :], AX.X, ALU.add))
            dl.link(V.tensor_scalar(keep[:, :], keep[:, :], -1.0, 2.0, ALU.mult, ALU.add))
            dl.link(V.memset(sx[:, :, :], -BIG))
            dl.link(V.memset(sr[:, :], -BIG))
            V.memset(acc[:, :], 0.0).then_inc(masks_ready, 1)
            dl.inc(V.memset(hd[0:H + 1, :], 0.0))
            dve.wait_ge(edge_turned, EG)
            dve.wait_ge(edge_saved[0], 48 * ((EG + 1) // 2))
            dve.wait_ge(edge_saved[1], 48 * (EG // 2))
            V.memset(oh[:, 0, 0, :], 0.0).then_inc(masks_ready, 1)
            dl.wait()
            prep_links = dl.n

            def mask_x(n, par):
                if not isinstance(n, int) or n >= 2:
                    dve.wait_ge(x_turned, n - 1)
                V.tensor_tensor(xm[:, par, :, :], xr[:, bass.ds(n, 1), :].to_broadcast([P, T, D]),
                                tmask[:, bass.ds(n, 1), :].rearrange("p a t -> p t a").to_broadcast([P, T, D]), ALU.mult)\
                 .then_inc(xm_ready, 1)

            def copy_tab(n, i, par):
                if not isinstance(n, int) or n >= 2:
                    dve.wait_ge(tab_saved[par], 16 * i)
                for k, (done, copied) in enumerate(((tab_k, k_copied), (tab_v, v_copied))):
                    dve.wait_ge(done, n + 1)
                    V.tensor_copy(stage[:, par, 0:GRP, k * D:(k + 1) * D],
                                  bank[4 + k][:, :].rearrange("p (r f) -> p r f", r=GRP)).then_inc(copied, 1)

            dve.wait_ge(x_in, 32)
            mask_x(0, 0)
            mask_x(1, 1)

            def table(n, i, par, peeled):
                mask_x(n + 2, par)
                copy_tab(n, i, par)
            steps_by_pairs(dve, 0, NT - 3, table)
            table(NT - 3, (NT - 3) // 2, (NT - 3) % 2, False)
            for n in (NT - 2, NT - 1):
                copy_tab(n, n // 2, n % 2)

            def one_hot_T(b, i, par, g):
                if g == 0:
                    dve.wait_ge(batch_in[par], 48 * (i + 1))
                if not (isinstance(b, int) and NG * b + g < 2):
                    dve.wait_ge(q_done, NG * b + g - 1)
                V.tensor_scalar(ohT[:, g % 2, :], relb[:, par, g * GRP * P:(g + 1) * GRP * P], iota_p[:, 0:1], None,
                                ALU.is_equal).then_inc(ohT_ready, 1)

            def logits(b, i, par, g):
                dve.wait_ge(kv_land[par][g], 64 * (i + 1))
                dve.wait_ge(q_done, NG * b + g + 1)
                kg = kv[:, par, g * GRP:(g + 1) * GRP, 0:D]
                dl.link(V.tensor_tensor(kg, kg, bank[g % 2][:, :].rearrange("p (s f) -> p s f", s=GRP), ALU.mult))
                if g == 0 and not (isinstance(b, int) and b == 0):
                    dve.wait_ge(logit_turned, b)
                V.tensor_reduce(logit[:, g * GRP * H:(g + 1) * GRP * H].rearrange("p (s h) -> p s h", h=H),
                                kg.rearrange("p s (h d) -> p s h d", d=DH), AX.X, ALU.add).then_inc(logit_done, 1)

            def ends(run, neg, k, at, signal):
                dl.inc(V.tensor_scalar(rhs[:, k, 0:TPB], tsel[:, :], run[:, at:at + 1], None, ALU.mult))
                dl.link(V.tensor_reduce(ini[:, 2:3], neg, AX.X, ALU.min))
                V.tensor_scalar(rhs[:, k, TPB:2 * TPB], tsel[:, :], ini[:, 2:3], None, ALU.mult).then_inc(signal, 1)
                dl.wait()

            def max_1(c, pc):
                dve.wait_ge(logit_turned, c + 1)
                if not (isinstance(c, int) and c == 0):
                    dve.wait_ge(dif_ready, c)
                dl.link(V.tensor_tensor_scan(mxf[:, :], negs[:, pc, 0, :], bank[2][:, 0:P], -BIG, ALU.add, ALU.max))
                ends(mxf, negs[:, pc, 0, :], 0, P - 1, fwd_ends)

            def max_2(c, pc):
                dve.wait_ge(fwd_chained, c + 1)
                dl.inc(V.tensor_copy(negall[:, 0, :], bank[3][0:H, TPB:2 * TPB]))
                if not (isinstance(c, int) and c == 0):
                    dve.wait_ge(fwd_carry, c)
                    dl.inc(V.tensor_copy(sx[:, pc, 0:1], sx[:, 1 - pc, TPB:TPB + 1]))
                dl.wait()
                V.tensor_tensor_scan(sx[:, pc, 1:TPB + 1], negall[:, 0, :], bank[3][0:H, 0:TPB], sx[:, pc, 0:1],
                                     ALU.add, ALU.max).then_inc(fwd_carry, 1)

            def initial(c, col, k):
                dl.link(V.tensor_tensor(tmp16[:, :], bank[3][:, col:col + TPB], tsel[:, :], ALU.mult))
                dl.link(V.tensor_reduce(ini[:, k:k + 1], tmp16[:, :], AX.X, ALU.add))

            def max_3(c, pc):
                dve.wait_ge(fwd_spread, c + 1)
                initial(c, 64, 0)
                dl.link(V.tensor_tensor_scan(mxf[:, :], negs[:, pc, 0, :], bank[2][:, 0:P], ini[:, 0:1], ALU.add, ALU.max))
                dl.link(V.tensor_tensor_scan(mxb[:, ::-1], negs[:, pc, 1, ::-1], mxf[:, ::-1], -BIG, ALU.add, ALU.max))
                ends(mxb, negs[:, pc, 1, :], 1, 0, bwd_ends)

            def max_4(c, pc):
                dve.wait_ge(bwd_chained, c + 1)
                dl.link(V.tensor_copy(negall[:, 1, :], bank[3][0:H, 128 + TPB:128 + 2 * TPB]))
                V.tensor_tensor_scan(sr[:, TPB - 1::-1], negall[:, 1, ::-1], bank[3][0:H, 128 + TPB - 1:127:-1], -BIG,
                                     ALU.add, ALU.max).then_inc(bwd_carry, 1)
                dve.wait_ge(bwd_carry, c + 1)
                dl.link(V.tensor_tensor(fd[:, :], sx[:, pc, 0:1], sr[:, 0:1], ALU.subtract))
                V.tensor_scalar(fd[:, :], fd[:, :], 0.0, None, ALU.min).then_inc(f_diff, 1)

            def max_5(c, pc):
                dve.wait_ge(bwd_spread, c + 1)
                initial(c, 192, 1)
                dl.link(V.tensor_tensor_scan(mxb[:, ::-1], negs[:, pc, 1, ::-1], mxf[:, ::-1], ini[:, 1:2], ALU.add, ALU.max))
                if not (isinstance(c, int) and c == 0):
                    dve.wait_ge(exT_ready, c)
                V.tensor_tensor(dif[:, :], bank[2][:, 0:P], mxb[:, :], ALU.subtract).then_inc(dif_ready, 1)

            def weigh(c, pc, g):
                first = isinstance(c, int) and NG * c + g < 2
                if not first:
                    dve.wait_ge(den_done, NG * c + g - 1)
                V.tensor_tensor(oh[:, g % 2, :, :], iota_j[:, :].rearrange("p (a j) -> p a j", a=1).to_broadcast([P, GRP, P]),
                                rel_c[:, bass.ds(c * TPB + g * GRP, GRP)].rearrange("p (s a) -> p s a", a=1)
                                .to_broadcast([P, GRP, P]), ALU.is_equal).then_inc(oh_ready, 1)
                if g == 0:
                    dve.wait_ge(exw_ready, c + 1)
                vg = kv[:, pc, g * GRP:(g + 1) * GRP, D:2 * D].rearrange("p s (h d) -> p s h d", d=DH)
                V.tensor_tensor(vg, vg, exw[:, g * GRP:(g + 1) * GRP, 0:H].rearrange("p s (h a) -> p s h a", a=1)
                                .to_broadcast([P, GRP, H, DH]), ALU.mult).then_inc(vw_ready, 1)

            def add_windows(c, g, firsts):
                if g == 0:
                    dve.wait_ge(f_spread, c + 1)
                    a_ = acc[:, bass.ds(firsts[0], 1)]
                    d_ = hd[0:H + 1, bass.ds(firsts[0], 1)]
                    if not (isinstance(c, int) and c == 0):
                        dve.wait_ge(acc_added, TPB * c)
                        dve.wait_ge(den_added, TPB * c)
                    V.tensor_tensor(a_, a_, bank[2][:, 2 * P:2 * P + 1], ALU.mult).then_inc(scaled, 1)
                    V.tensor_tensor(d_, d_, f9[:, :], ALU.mult).then_inc(scaled, 1)
                    dve.wait_ge(scaled, 2 * c + 2)
                for s in range(GRP):
                    t = g * GRP + s
                    if s == 0:
                        dve.wait_ge(agg_done, NG * c + g + 1)
                    for o_, d_, added in ((acc, bank[4 + g % 2], acc_added), (hd, bank[6 + g % 2], den_added)):
                        n = P if o_ is acc else H + 1
                        if s == 0 and o_ is hd:
                            dve.wait_ge(den_done, NG * c + g + 1)
                        if not (isinstance(c, int) and c == 0 and t == 0):
                            dve.wait_ge(added, TPB * c + t)
                        w_ = o_[0:n, bass.ds(firsts[s], P)]
                        V.tensor_tensor(w_, w_, d_[0:n, s * P:(s + 1) * P], ALU.add).then_inc(added, 1)

            def window_starts(c, g):
                return load_starts(c * TPB + g * GRP)

            def weigh_and_add(c, pc, g):
                if g < NG:
                    weigh(c, pc, g)
                if g >= 1:
                    add_windows(c, g - 1, window_starts(c, g - 1))

            counts = {}

            def attend(b, i, par, peeled):
                c, pc = b - 1, 1 - par
                if isinstance(b, int) and b == 0:
                    dl.at(prep_links)
                    one_hot_T(b, i, par, 0)
                    for g in range(NG):
                        if g + 1 < NG:
                            one_hot_T(b, i, par, g + 1)
                        logits(b, i, par, g)
                    counts["after0"] = prep_links + dl.n
                    return
                if "step" in counts:
                    dl.at(counts["after1"] + counts["step"] * (b - 2))
                else:
                    dl.at(counts["after1"] if "after1" in counts else counts["after0"])
                one_hot_T(b, i, par, 0)
                one_hot_T(b, i, par, 1)
                max_1(c, pc)
                max_2(c, pc)
                logits(b, i, par, 0)
                max_3(c, pc)
                one_hot_T(b, i, par, 2)
                max_4(c, pc)
                logits(b, i, par, 1)
                one_hot_T(b, i, par, 3)
                max_5(c, pc)
                weigh_and_add(c, pc, 0)
                weigh_and_add(c, pc, 1)
                logits(b, i, par, 2)
                weigh_and_add(c, pc, 2)
                weigh_and_add(c, pc, 3)
                weigh_and_add(c, pc, 4)
                logits(b, i, par, 3)
                if "after1" not in counts:
                    counts["after1"] = counts["after0"] + dl.n
                elif "step" not in counts:
                    counts["step"] = dl.n
                else:
                    assert counts["step"] == dl.n
            attend(0, 0, 0, True)
            attend(1, 0, 1, True)
            counts["step"] = dl.n + 1
            with dve.Fori(1, NB // 2) as i:
                for par in (0, 1):
                    attend(2 * i + par, i, par, False)
            c, pc = NB - 1, 1
            dl.at(counts["after1"] + counts["step"] * (NB - 2))
            max_1(c, pc)
            max_2(c, pc)
            max_3(c, pc)
            max_4(c, pc)
            max_5(c, pc)
            for g in range(NG + 1):
                weigh_and_add(c, pc, g)
            dl.at(dl.base + dl.n)
            yr = big[:, 0:NP_].rearrange("p (n f) -> p n f", f=D)

            dve.wait_ge(den_turned, 1)
            dl.link(V.tensor_scalar(nodec[:, :, 0:H], bank[0][:, 0:NT * (H + 1)].rearrange("p (n h) -> p n h", h=H + 1)[:, :, 0:H],
                                    1e-9, None, ALU.max))
            V.tensor_scalar(nodec[:, :, H], bank[0][:, 0:NT * (H + 1)].rearrange("p (n h) -> p n h", h=H + 1)[:, :, H],
                            1.0, 1e-30, ALU.add, ALU.max).then_inc(deg_ready, 1)
            dve.wait_ge(root_ready, 1)
            V.reciprocal(nodec[:, :, :], nodec[:, :, :]).then_inc(deg_ready, 1)
            dve.wait_ge(deg_ready, 2)
            V.scalar_tensor_tensor(out=nodec[:, :, H], in0=nodec[:, :, H], scalar=5e14, in1=nodec[:, :, H],
                                   op0=ALU.is_lt, op1=ALU.mult).then_inc(deg_ready, 1)
            for c, (c0, cw) in enumerate(CH):
                dve.wait_ge(den_spread, c + 1)
                if c == 0:
                    dve.wait_ge(acc_added, ET)
                V.tensor_tensor(acc[:, c0:c0 + cw], acc[:, c0:c0 + cw], bank[1 + c % 3][:, 0:cw], ALU.mult).then_inc(attn_scaled, 1)
            V.tensor_tensor(yr, xr[:, :, :], keep[:, :].rearrange("p (n a) -> p n a", a=1).to_broadcast([P, NT, D]),
                            ALU.mult).then_inc(y_set, 1)
            dve.wait_ge(y_set, 1)

            def y_rows(i, tiles):
                dve.wait_ge(types_done, 2 * i + len(tiles))
                per = len(tiles)
                for t in range(T):
                    for k in tiles:
                        if t:
                            dve.wait_ge(y_sum, 8 * i + per * (t - 1) + k + 1)
                        y_ = big[:, bass.ds((2 * i + k) * D, D)]
                        V.scalar_tensor_tensor(out=y_, in0=bank[4 + k][:, t * D:(t + 1) * D],
                                               scalar=gmask[:, bass.ds(2 * i + k, 1), t:t + 1].rearrange("p a t -> p (a t)"),
                                               in1=y_, op0=ALU.mult, op1=ALU.add).then_inc(y_sum, 1)
                for k in tiles:
                    dve.wait_ge(y_sum, 8 * i + per * (T - 1) + k + 1)
                    V.bn_stats(bst[:, bass.ds(2 * i + k, 1), :].rearrange("p a s -> p (a s)"), big[:, bass.ds((2 * i + k) * D, D)])\
                     .then_inc(stat_done, 1)
            with dve.Fori(0, NT // 2) as i:
                y_rows(i, (0, 1))
            y_rows(NT // 2, (0,))

            def row_moments(k):
                dve.wait_ge(stat_done, NT * k)
                dl.inc(V.tensor_tensor(mv[:, :, 0], bst[:, :, 1], bst[:, :, 4], ALU.add))
                dl.inc(V.tensor_tensor(mv[:, :, 1], bst[:, :, 1], bst[:, :, 4], ALU.subtract))
                dl.link(V.tensor_tensor(bst[:, :, 0], bst[:, :, 2], bst[:, :, 5], ALU.add))
                dl.inc(V.tensor_scalar(mv[:, :, 0], mv[:, :, 0], 0.5, None, ALU.mult))
                dl.inc(V.tensor_scalar(bst[:, :, 0], bst[:, :, 0], 1.0 / D, None, ALU.mult))
                dl.link(V.scalar_tensor_tensor(out=mv[:, :, 1], in0=mv[:, :, 1], scalar=0.25, in1=mv[:, :, 1],
                                               op0=ALU.mult, op1=ALU.mult))
                V.tensor_tensor(mv[:, :, 1], mv[:, :, 1], bst[:, :, 0], ALU.add).then_inc(var_ready, 1)
                dve.wait_ge(std_ready, {1: 1, 2: 2, 3: 6}[k])
                dl.link(V.reciprocal(rs[:, :], rs[:, :]))

            def negated_shift(k):
                V.scalar_tensor_tensor(out=shf[:, :], in0=mv[:, :, 0], scalar=-1.0, in1=rs[:, :], op0=ALU.mult, op1=ALU.mult)\
                 .then_inc(shift_ready, 1)

            row_moments(1)
            negated_shift(1)
            dve.wait_ge(xb_ready, 1)
            for c, (c0, cw) in enumerate(CH):
                n0, n1 = c0 // P, (c0 + cw) // P
                dve.wait_ge(y_normed, n1)
                y_ = yr[:, n0:n1, :]
                dl.link(V.tensor_tensor(y_, y_, lnw[:, 0:1, :].to_broadcast([P, n1 - n0, D]), ALU.mult))
                dl.link(V.tensor_tensor(y_, y_, xr[:, n0:n1, :], ALU.add))
                for n in range(n0, n1):
                    V.bn_stats(bst[:, n, :], yr[:, n, :]).then_inc(stat_done, 1)
            row_moments(2)
            negated_shift(2)

            for l in range(3):
                for c, (c0, cw) in enumerate(CH):
                    if l == 0:
                        dve.wait_ge(x1_turned, c + 1)
                        V.tensor_copy(big[:, c0:c0 + cw], bank[c % 2][:, 0:cw]).then_inc(dinv_ready, 1)
                        dve.wait_ge(dinv_ready, c + 1)
                        V.tensor_tensor(acc[:, c0:c0 + cw], bank[2 + c % 2][:, 0:cw], big[:, c0:c0 + cw], ALU.mult).then_inc(acc_set, 1)
                    else:
                        dve.wait_ge(act_ready, NCH * (l - 1) + c + 1)
                        V.tensor_tensor(acc[:, c0:c0 + cw], hd[:, c0:c0 + cw], big[:, c0:c0 + cw], ALU.mult).then_inc(acc_set, 1)
                dve.wait_ge(rows_turned, NCH * (l + 1))
                dve.wait_ge(acc_set, NCH * (l + 1))

                def weigh(B, b, g, s):
                    if s == 0 and not (isinstance(B, int) and NG * B + g < NG):
                        dve.wait_ge(sum_done, NG * B + g - 3)
                    t_ = b * TPB + (g * GRP + s)
                    V.tensor_scalar(oh[:, g, s, :], iota_j[:, :], rel_c[:, bass.ds(t_, 1)], ew_c[:, bass.ds(t_, 1)],
                                    ALU.is_equal, ALU.mult).then_inc(wt_ready, 1)

                def windows(b, i, par, peeled):
                    B = b + NB * l
                    last = isinstance(b, int) and b == NB - 1
                    for g in range(NG):
                        firsts = load_starts(b * TPB + g * GRP)
                        for s in range(GRP):
                            if g < 2:
                                weigh(B, b, g + 2, s)
                            elif not last:
                                weigh(B + 1, b + 1, g - 2, s)
                            t = g * GRP + s
                            if s == 0:
                                dve.wait_ge(sum_done, NG * B + g + 1)
                            if not (isinstance(B, int) and B == 0 and t == 0):
                                dve.wait_ge(win_added, TPB * B + t)
                            w_ = acc[:, bass.ds(firsts[s], P)]
                            V.tensor_tensor(w_, w_, bank[g][:, s * P:(s + 1) * P], ALU.add).then_inc(win_added, 1)
                for g in range(2):
                    for s in range(GRP):
                        weigh(NB * l, 0, g, s)
                steps_by_pairs(dve, 0, NB, windows, tail=2)

                for c, (c0, cw) in enumerate(CH):
                    dve.wait_ge(lin_done, NCH * l + c + 1)
                    V.tensor_tensor(hd[:, c0:c0 + cw], bank[c % 4][:, 0:cw], big[:, c0:c0 + cw], ALU.mult).then_inc(h_scaled, 1)
                for c, (c0, cw) in enumerate(CH):
                    dve.wait_ge(h_ready, NCH * l + c + 1)
                    dl.inc(V.bn_stats(bst[:, c, :], hd[:, c0:min(c0 + cw, N)]))
                dl.wait()
                V.bn_aggr(mv[:, 0, :], bst[:, 0:NCH, :].rearrange("p c s -> p (c s)")).then_inc(var_ready, 1)
                dve.wait_ge(std_ready, 3 + l)
                dl.link(V.reciprocal(rs[:, 0:1], rs[:, 0:1]))
                dl.link(V.tensor_tensor(bn[:, 0:1], rs[:, 0:1], gcnv[:, 3 + l:4 + l], ALU.mult))
                dl.link(V.tensor_tensor(bn[:, 2:3], mv[:, 0, 0:1], bn[:, 0:1], ALU.mult))
                V.tensor_tensor(bn[:, 1:2], gcnv[:, 6 + l:7 + l], bn[:, 2:3], ALU.subtract).then_inc(bn_ready, 1)

            for c, (c0, cw) in enumerate(CH):
                dve.wait_ge(h_turned, c + 1)
                x_ = xr[:, c0 // P:(c0 + cw) // P, :]
                V.tensor_tensor(x_, x_, bank[4 + c % 4][:, 0:cw].rearrange("p (t f) -> p t f", f=D), ALU.add).then_inc(res_added, 1)
            dve.wait_ge(res_added, NCH)
            with dve.Fori(0, NT) as n:
                V.bn_stats(bst[:, bass.ds(n, 1), :].rearrange("p a s -> p (a s)"),
                           xr[:, bass.ds(n, 1), :].rearrange("p a f -> p (a f)")).then_inc(stat_done, 1)
            row_moments(3)
            with dve.Fori(0, NT) as n:
                x_ = xr[:, bass.ds(n, 1), :].rearrange("p a f -> p (a f)")
                V.tensor_scalar(x_, x_, mv[:, bass.ds(n, 1), 0], rs[:, bass.ds(n, 1)], ALU.subtract, ALU.mult)\
                 .then_inc(out_ready, 1)
    return nc


_INS = ["x", "src", "dst", "edge_type_6", "edge_weight", "node_type_4", "L0_gnn_Wk", "L0_gnn_Wq", "L0_gnn_Wv",
        "L0_gnn_Wa", "L0_gnn_rel_pri", "L0_gnn_rel_att", "L0_gnn_rel_msg", "L0_gnn_skip", "L0_gnn_ln_gamma",
        "L0_gnn_ln_beta", "L1_gnn_W1", "L1_gnn_b1", "L1_gnn_W2", "L1_gnn_b2", "L1_gnn_W3", "L1_gnn_b3",
        "L1_gnn_g1", "L1_gnn_be1", "L1_gnn_g2", "L1_gnn_be2", "L1_gnn_g3", "L1_gnn_be3"]


def kernel(**inputs):
    import numpy as _np
    import concourse.bacc as _bacc
    from concourse import mybir as _mybir
    from concourse.bass_utils import run_bass_kernel_spmd as _run

    nc = _bacc.Bacc("TRN2", target_bir_lowering=False, num_devices=1)
    arrays, args = {}, []
    for name in _INS:
        a = _np.ascontiguousarray(inputs[name])
        arrays[f"in_{name}"] = a
        args.append(nc.dram_tensor(f"in_{name}", a.shape, _mybir.dt.from_np(a.dtype), kind="ExternalInput").ap())
    shape = arrays["in_x"].shape
    args.append(nc.dram_tensor("out_0", shape, _mybir.dt.from_np(_np.dtype("float32")), kind="ExternalOutput").ap())
    gnn(nc, *args)
    r = _run(nc, [arrays], core_ids=[0])
    return r.results[0]["out_0"]
```

```python
from contextlib import ExitStack

import concourse.bass as bass
from concourse import mybir

F32 = mybir.dt.float32
BF16 = mybir.dt.bfloat16
I32 = mybir.dt.int32
ALU = mybir.AluOpType
ACT = mybir.ActivationFunctionType
AX = mybir.AxisListType

P = 128
BIG = 1.0e30
PAD_DST = 20000
EPS = 1e-5
TPB = 16
GRP = 4
NG = TPB // GRP


def steps_by_pairs(eng, first, last, step, tail=0):
    for n in range(first, 2):
        step(n, n // 2, n % 2, True)
    with eng.Fori(1, (last - tail) // 2) as i:
        for par in (0, 1):
            step(2 * i + par, i, par, False)
    for n in range(2 * ((last - tail) // 2), last):
        step(n, n // 2, n % 2, False)


class Links:

    def __init__(self, eng, sem):
        self.eng, self.sem, self.n, self.base = eng, sem, 0, 0

    def at(self, base):
        self.base, self.n = base, 0

    def inc(self, ins):
        self.n += 1
        ins.then_inc(self.sem, 1)

    def wait(self, back=0):
        self.eng.wait_ge(self.sem, self.base + (self.n - back))

    def link(self, ins):
        self.inc(ins)
        self.wait()


def gnn(nc, x, src, dst, etype, ew, ntype, Wk, Wq, Wv, Wa, rel_pri, rel_att, rel_msg, skip, gamma, beta,
        W1, b1, W2, b2, W3, b3, g1, be1, g2, be2, g3, be3, out):
    N, D = x.shape
    E = src.shape[0]
    T = Wk.shape[0]
    H, R = rel_pri.shape
    DH = D // H
    assert D == P and TPB * H == P and D // DH == H
    NT = -(-N // P)
    NF = N // P
    NR = N - NF * P
    NP_ = NT * P
    NW = NP_ + P
    ET = -(-E // (P * TPB)) * TPB
    NB = ET // TPB
    EG = -(-ET // P)
    EFULL = (E // (P * P)) * P * P
    GF = EFULL // (P * P)
    TR = (E - EFULL) // P
    ER = E - EFULL - TR * P
    assert EG == GF + 1 and NR > 0 and ER > 0 and NT % 2 == 1 and NB % 2 == 0
    CH = [(c, min(512, NP_ - c)) for c in range(0, NP_, 512)]
    NCH = len(CH)

    kv_tab = nc.dram_tensor("kv_tab", (N * R, 2 * D), F32, kind="Internal").ap()
    q_tab = nc.dram_tensor("q_tab", (NW, D), F32, kind="Internal").ap()
    h_tab = [nc.dram_tensor(f"h_tab{i}", (N, D), F32, kind="Internal").ap() for i in range(3)]
    rel_d = nc.dram_tensor("rel_d", (EG * P * P,), BF16, kind="Internal").ap()
    negf_d = nc.dram_tensor("negf_d", (EG * P * H, P), F32, kind="Internal").ap()
    negb_d = nc.dram_tensor("negb_d", (EG * P * H, P), F32, kind="Internal").ap()

    with ExitStack() as ctx:
        def sb(name, shape, dt=F32):
            return ctx.enter_context(nc.sbuf_tensor(name, shape, dt))

        def sem(name):
            return ctx.enter_context(nc.semaphore(name))

        bank = [ctx.enter_context(nc.psum_tensor(f"bank{i}", [P, 512], F32)) for i in range(8)]

        xr = sb("xr", [P, NT, D])
        sums2 = sb("sums2", [P, 2, NW])
        acc = sums2[:, 0, :]
        hd = sums2[:, 1, :]
        earr = sb("earr", [P, 4, EG * P])
        rel_c, idx_c, src_c, ew_c = (earr[:, k, :] for k in range(4))
        base_row = sb("base_row", [1, ET], I32)
        big = sb("big", [P, 2 * TPB * 2 * D])
        kv = big[:, :].rearrange("p (a t f) -> p a t f", a=2, t=TPB)
        relb = sb("relb", [P, 2, TPB * P], BF16)
        negs = sb("negs", [P, 2, 2, P])
        qwin = sb("qwin", [P, TPB, D])
        ohT = sb("ohT", [P, 2, GRP * P])
        oh = sb("oh", [P, NG, GRP, P])
        stage = sb("stage", [P, 2, R, 2 * D])
        gring = stage[:, :, :, :].rearrange("p a r f -> p (a r f)")[:, 0:TPB * D].rearrange("p (t f) -> p t f", t=TPB)
        exw = stage[:, :, :, :].rearrange("p a r f -> p (a r f)")[:, 0:TPB * P].rearrange("p (t f) -> p t f", t=TPB)
        bd = sb("bd", [P, 2, R, D])
        wkqv = sb("wkqv", [P, 3, T, D])
        wa = sb("wa", [P, T, D])
        wg = sb("wg", [P, 3, D])
        xmT = sb("xmT", [P, 2, 2, T, D])
        xm, xT = xmT[:, 0, :, :, :], xmT[:, 1, :, :, :]
        vw = xmT[:, :, :, :, :].rearrange("p k a t f -> p (k a t) f")
        qkv = sb("qkv", [P, 2, 3, D])
        idxr = sb("idxr", [P, 2, TPB], I32)
        logit = sb("logit", [P, P])
        mxf = sb("mxf", [P, P])
        mxb = sb("mxb", [P, P])
        dif = sb("dif", [P, P])
        exT = sb("exT", [P, P])
        rhs = sb("rhs", [P, 2, 2 * TPB])
        sx = sb("sx", [H, 2, TPB + 1])
        sr = sb("sr", [H, TPB + 1])
        negall = sb("negall", [H, 2, TPB])
        ini = sb("ini", [P, 4])
        tmp16 = sb("tmp16", [P, TPB])
        nodec = sb("nodec", [P, NT, H + 1])
        shf = sb("shf", [P, NT])
        fd = sb("fd", [H, 1])
        f9 = sb("f9", [H + 1, 1])
        iota_j = sb("iota_j", [P, P])
        iota_p = sb("iota_p", [P, 1])
        ident = sb("ident", [P, P])
        tsel = sb("tsel", [P, TPB])
        hselT = sb("hselT", [H, P])
        hsel = sb("hsel", [P, H])
        fsel = sb("fsel", [H + 1, P])
        dsel = sb("dsel", [H + 1, P])
        pri = sb("pri", [P, R])
        nti = sb("nti", [NT, P], I32)
        ntf = sb("ntf", [NT, P])
        nt_c = sb("nt_c", [P, NT])
        tmask = sb("tmask", [P, NT, T])
        gmask = sb("gmask", [P, NT, T])
        keep = sb("keep", [P, NT])
        sk = sb("sk", [P, 3, T])
        lnw = sb("lnw", [P, 2, D])
        gcnv = sb("gcnv", [P, 9])
        bst = sb("bst", [P, NT, 6])
        mv = sb("mv", [P, NT, 2])
        rs = sb("rs", [P, NT])
        bn = sb("bn", [P, 4])
        epsc = sb("epsc", [P, 2])

        ei = big[:, 0:EG * 5 * P].bitcast(I32).rearrange("p (g k e) -> p g k e", g=EG, k=5)
        o = EG * 5 * P
        ewi = big[:, o:o + EG * P].rearrange("p (g e) -> p g e", g=EG)
        o += EG * P
        ef = big[:, o:o + 2 * 4 * P].rearrange("p (a k e) -> p a k e", a=2, k=4)
        o += 2 * 4 * P
        assert o <= big.shape[1]
        nb = ohT[:, :, :].rearrange("p a (k e) -> p a k e", k=4)
        ro = oh[:, :, :, :]
        relw = qwin[:, 0:2 * GRP, :].rearrange("p a f -> p (a f)").bitcast(BF16).rearrange("p (a e) -> p a e", a=16)

        pads_set = sem("pads_set")
        edges_in = sem("edges_in")
        weights_in = sem("weights_in")
        x_in = sem("x_in")
        const_link = sem("const_link")
        consts_ready = sem("consts_ready")
        edge_rows = sem("edge_rows")
        edge_turned = sem("edge_turned")
        edge_cols = sem("edge_cols")
        edge_saved = [sem(f"edge_saved{a}") for a in range(2)]
        dve_link = sem("dve_link")
        nt_ready, nt_turned, hsel_turned, masks_ready, hsel_ready = (
            sem(n) for n in ("nt_ready", "nt_turned", "hsel_turned", "masks_ready", "hsel_ready"))
        skip_exp = sem("skip_exp")
        xm_ready, x_turned, xT_ready, qkv_done, qkv_ready, tab_k, tab_v, tab_kv, k_copied, v_copied, kv_copied = (
            sem(n) for n in ("xm_ready", "x_turned", "xT_ready", "qkv_done", "qkv_ready", "tab_k", "tab_v",
                             "tab_kv", "k_copied", "v_copied", "kv_copied"))
        tab_saved = [sem(f"tab_saved{a}") for a in range(2)]
        q_saved = [sem(f"q_saved{a}") for a in range(2)]
        zeros_saved = sem("zeros_saved")
        tabs_complete = sem("tabs_complete")
        idx_ready = sem("idx_ready")
        gathers_begun = sem("gathers_begun")
        kv_land = [[sem(f"kv_land{a}_{g}") for g in range(NG)] for a in range(2)]
        rel_in = [sem(f"rel_in{a}") for a in range(2)]
        neg_in = [sem(f"neg_in{a}") for a in range(2)]
        act_link = sem("act_link")
        exw_zero = sem("exw_zero")
        qwin_in = [sem(f"qwin_in{g}") for g in range(NG)]
        ohT_ready, q_done, logit_done, logit_turned = (
            sem(n) for n in ("ohT_ready", "q_done", "logit_done", "logit_turned"))
        flags_ready = sem("flags_ready")
        fwd_ends, fwd_chained, fwd_carry, fwd_spread = (
            sem(n) for n in ("fwd_ends", "fwd_chained", "fwd_carry", "fwd_spread"))
        bwd_ends, bwd_chained, bwd_carry, bwd_spread = (
            sem(n) for n in ("bwd_ends", "bwd_chained", "bwd_carry", "bwd_spread"))
        f_diff, f_ready, dif_ready, exT_ready, ex_turned, exw_ready = (
            sem(n) for n in ("f_diff", "f_ready", "dif_ready", "exT_ready", "ex_turned", "exw_ready"))
        vw_ready, oh_ready, agg_done, acc_added = (
            sem(n) for n in ("vw_ready", "oh_ready", "agg_done", "acc_added"))
        scaled, f_spread, ewcol_ready = (sem(n) for n in ("scaled", "f_spread", "ewcol_ready"))
        den_spread, attn_scaled, types_done, y_sum, y_normed, x1_ready, deg_ready, root_ready, dinv_ready = (
            sem(n) for n in ("den_spread", "attn_scaled", "types_done", "y_sum", "y_normed", "x1_ready",
                             "deg_ready", "root_ready", "dinv_ready"))
        var_ready, std_ready, stat_done, shift_ready, y_set, xb_ready, den_turned, den_wide = (
            sem(n) for n in ("var_ready", "std_ready", "stat_done", "shift_ready", "y_set", "xb_ready", "den_turned", "den_wide"))
        x1_turned, acc_set, rows_turned, rows_ready, tab_complete = (
            sem(n) for n in ("x1_turned", "acc_set", "rows_turned", "rows_ready", "tab_complete"))
        rows_saved = [sem(f"rows_saved{a}") for a in range(2)]
        src_ready = sem("src_ready")
        row_land = [sem(f"row_land{g}") for g in range(NG)]
        wt_ready, sum_done, win_added, lin_done, h_scaled, h_ready, bn_ready, act_ready, h_turned = (
            sem(n) for n in ("wt_ready", "sum_done", "win_added", "lin_done", "h_scaled", "h_ready", "bn_ready",
                             "act_ready", "h_turned"))
        res_added, out_ready, out_saved = (sem(n) for n in ("res_added", "out_ready", "out_saved"))

        loads = []
        per_group = lambda a: a.rearrange("(g p e) -> p g e", p=P, e=P)
        for k, a in ((0, dst), (3, src), (4, etype)):
            loads.append((ei[:, 0:GF, k, :], per_group(a[0:EFULL])))
            loads.append((ei[0:TR, GF, k, :], a[EFULL:EFULL + TR * P].rearrange("(p e) -> p e", e=P)))
            loads.append((ei[TR:TR + 1, GF, k, 0:ER], a[EFULL + TR * P:E].rearrange("(p e) -> p e", p=1)))
        loads.append((ewi[:, 0:GF, :], per_group(ew[0:EFULL])))
        loads.append((ewi[0:TR, GF, :], ew[EFULL:EFULL + TR * P].rearrange("(p e) -> p e", e=P)))
        loads.append((ewi[TR:TR + 1, GF, 0:ER], ew[EFULL + TR * P:E].rearrange("(p e) -> p e", p=1)))
        loads.append((ei[:, 1:GF, 1, :], per_group(dst[P * P - 1:EFULL - 1])))
        loads.append((ei[1:P, 0, 1, :], dst[P - 1:P * P - 1].rearrange("(p e) -> p e", e=P)))
        loads.append((ei[0:1, 0, 1, 1:P], dst[0:P - 1].rearrange("(p e) -> p e", p=1)))
        loads.append((ei[0:TR, GF, 1, :], dst[EFULL - 1:EFULL - 1 + TR * P].rearrange("(p e) -> p e", e=P)))
        loads.append((ei[TR:TR + 1, GF, 1, 0:ER + 1], dst[EFULL + TR * P - 1:E].rearrange("(p e) -> p e", p=1)))
        loads.append((ei[:, 0:GF, 2, :], per_group(dst[1:EFULL + 1])))
        loads.append((ei[0:TR, GF, 2, :], dst[EFULL + 1:EFULL + 1 + TR * P].rearrange("(p e) -> p e", e=P)))
        loads.append((ei[TR:TR + 1, GF, 2, 0:ER - 1], dst[EFULL + TR * P + 1:E].rearrange("(p e) -> p e", p=1)))
        NFULL = E // P
        loads.append((base_row[0:1, 0:NFULL], dst[0:NFULL * P].rearrange("(a t e) -> a t e", a=1, e=P)[:, :, 0]))
        loads.append((base_row[0:1, NFULL:NFULL + 1], dst[NFULL * P:NFULL * P + 1].rearrange("(a t) -> a t", a=1)))

        row = lambda v: v.rearrange("(a n) -> a n", a=1)
        wloads = [(nti[0:NF, :], ntype[0:NF * P].rearrange("(t p) -> t p", p=P)),
                  (nti[NF:NT, 0:NR], row(ntype[NF * P:N])),
                  (sk[:, 0, :], row(skip).to_broadcast([P, T])),
                  (lnw[:, 0, :], row(gamma).to_broadcast([P, D])),
                  (lnw[:, 1, :], row(beta).to_broadcast([P, D])),
                  (wa[:, :, :], Wa.rearrange("t i o -> i t o"))]
        for k, w in enumerate((Wq, Wk, Wv)):
            wloads.append((wkqv[:, k, :, :], w.rearrange("t i o -> i t o")))
        for k, w in enumerate((W1, W2, W3)):
            wloads.append((wg[:, k, :], w))
        for k, v in enumerate((b1, b2, b3, g1, g2, g3, be1, be2, be3)):
            wloads.append((gcnv[:, k:k + 1], v.rearrange("(p a) -> p a", a=1)))
        for h in range(H):
            rows = slice(h * DH, (h + 1) * DH)
            wloads.append((pri[rows, :], rel_pri[h:h + 1, :].to_broadcast([DH, R])))
            for k, w in enumerate((rel_att, rel_msg)):
                wloads.append((bd[rows, k, :, h * DH:(h + 1) * DH], w[h].rearrange("r i o -> i r o")))
        PADS = 11

        block = ctx.enter_context(nc.Block())

        def load_starts(engine, t):
            return nc.values_load_multi_w_load_instructions(
                base_row[0:1, bass.ds(t, GRP)], engines=[engine], min_val=0, max_val=N - 1,
                skip_runtime_bounds_check_because="the destinations are node numbers, and nothing else writes here")[1]

        @block.sync
        def _(sp):
            sp.wait_ge(pads_set, PADS)
            with nc.allow_non_contiguous_dma(reason="short columns"):
                for o_, i_ in loads:
                    sp.dma_start(o_, i_).then_inc(edges_in, 16)
                for o_, i_ in wloads:
                    sp.dma_start(o_, i_).then_inc(weights_in, 16)
            sp.dma_start(xr[:, 0:NF, :], x[0:NF * P, :].rearrange("(i p) f -> p i f", p=P)).then_inc(x_in, 16)
            sp.dma_start(xr[0:NR, NF, :], x[NF * P:N, :]).then_inc(x_in, 16)

            for g in range(EG):
                n = min(P, ET - g * P)
                sp.wait_ge(edge_rows, g + 1)
                sp.dma_start(rel_d[g * P * P:g * P * P + n * P].rearrange("(p e) -> p e", e=P),
                             relw[0:n, g % 2, :]).then_inc(edge_saved[g % 2], 16)
                for k, d in enumerate((negf_d, negb_d)):
                    sp.dma_start(d[g * P * H:(g * P + n) * H, :].rearrange("(p h) e -> p h e", h=H),
                                 nb[0:n, g % 2, k:k + 1, :].to_broadcast([n, H, P])).then_inc(edge_saved[g % 2], 16)

            def save(n, i, par, peeled):
                rows = NR if (isinstance(n, int) and n == NF) else P
                sp.wait_ge(k_copied, n + 1)
                sp.wait_ge(v_copied, n + 1)
                sp.wait_ge(kv_copied, n + 1)
                tab = kv_tab.rearrange("(n r) f -> n (r f)", r=R)
                sp.dma_start(tab[bass.ds(n * P, rows), :],
                             stage[0:rows, par, :, :].rearrange("p r f -> p (r f)")).then_inc(tab_saved[par], 16)
                sp.dma_start(q_tab[bass.ds(n * P, P), :], qkv[:, par, 0, :]).then_inc(q_saved[par], 16)
            steps_by_pairs(sp, 0, NT, save)
            sp.wait_ge(masks_ready, 2)
            sp.dma_start(q_tab[NP_:NW, :], oh[:, 0, 0, :]).then_inc(zeros_saved, 16)
            for a in range(2):
                cnt = (NT + 1 - a) // 2
                sp.wait_ge(tab_saved[a], 16 * cnt)
                sp.wait_ge(q_saved[a], 16 * cnt)
            sp.wait_ge(zeros_saved, 16)
            for a in range(2):
                sp.wait_ge(edge_saved[a], 48 * ((EG + 1 - a) // 2))
            sp.sem_inc(tabs_complete, 1)

            def feed(b, i, par, peeled):
                if not peeled:
                    sp.wait_ge(ohT_ready, NG * (b - 1))
                sp.dma_start(relb[:, par, :], rel_d[bass.ds(b * (TPB * P), TPB * P)].rearrange("(a n) -> a n", a=1)
                             .to_broadcast([P, TPB * P])).then_inc(rel_in[par], 16)
                for g in range(NG):
                    firsts = load_starts(mybir.EngineType.SP, b * TPB + g * GRP)
                    if g == 2 and not peeled:
                        sp.wait_ge(logit_turned, b)
                    elif not (isinstance(b, int) and b == 0):
                        sp.wait_ge(q_done, NG * (b - 1) + g + 1)
                    for s in range(GRP):
                        sp.dma_start(qwin[:, g * GRP + s, :], q_tab[bass.ds(firsts[s], P), :]).then_inc(qwin_in[g], 16)
                    if g == 2:
                        sp.dma_start(negs[:, par, 0, :], negf_d[bass.ds(b * P, P), :]).then_inc(neg_in[par], 16)
                        sp.dma_start(negs[:, par, 1, :], negb_d[bass.ds(b * P, P), :]).then_inc(neg_in[par], 16)
            steps_by_pairs(sp, 0, NB, feed)

            for l in range(3):
                for c, (c0, cw) in enumerate(CH):
                    sp.wait_ge(rows_ready, NCH * l + c + 1)
                    rows, tiles = min(cw, N - c0), cw // P
                    a = (NCH * l + c) % 2
                    if rows == cw:
                        sp.dma_start(h_tab[l][c0:c0 + rows, :].rearrange("(i p) f -> p i f", p=P),
                                     xT[:, a, 0:tiles, :]).then_inc(rows_saved[a], 16)
                    else:
                        assert tiles == 1
                        sp.dma_start(h_tab[l][c0:N, :], xT[0:rows, a, 0, :]).then_inc(rows_saved[a], 16)
                for a in range(2):
                    sp.wait_ge(rows_saved[a], 16 * ((NCH * (l + 1) + 1 - a) // 2))
                sp.sem_inc(tab_complete, 1)
            for c, (c0, cw) in enumerate(CH):
                sp.wait_ge(out_ready, c0 // P + cw // P)
                if c0 + cw <= N:
                    sp.dma_start(out[c0:c0 + cw, :].rearrange("(i p) f -> p i f", p=P),
                                 xr[:, c0 // P:(c0 + cw) // P, :]).then_inc(out_saved, 16)
                else:
                    sp.dma_start(out[c0:N, :], xr[0:N - c0, c0 // P, :]).then_inc(out_saved, 16)
            sp.wait_ge(out_saved, 16 * NCH)

        @block.gpsimd
        def _(pool):
            G = nc.gpsimd
            link = Links(pool, const_link)
            G.iota(iota_j[:], [[1, P]], base=0, channel_multiplier=0, allow_small_or_imprecise_dtypes=True).then_inc(consts_ready, 1)
            G.iota(iota_p[:], [[1, 1]], base=0, channel_multiplier=1, allow_small_or_imprecise_dtypes=True).then_inc(consts_ready, 1)
            for t_, v_ in ((ident, 0.0), (hselT, 0.0), (fsel, 0.0), (dsel, 0.0), (tsel, 1.0)):
                link.inc(G.memset(t_[:, :], v_))
            link.wait()
            G.affine_select(out=ident[:, :], in_=ident[:, :], compare_op=ALU.not_equal, fill=1.0, base=0,
                            pattern=[[-1, P]], channel_multiplier=1).then_inc(consts_ready, 1)
            v_ = hselT[:, :].rearrange("h (t g) -> h t g", g=H)
            G.affine_select(out=v_, in_=v_, compare_op=ALU.not_equal, fill=1.0, base=0,
                            pattern=[[0, TPB], [1, H]], channel_multiplier=-1).then_inc(consts_ready, 1)
            v_ = fsel[:, :].rearrange("h (g d) -> h g d", d=DH)
            G.affine_select(out=v_, in_=v_, compare_op=ALU.not_equal, fill=1.0, base=0,
                            pattern=[[1, H], [0, DH]], channel_multiplier=-1).then_inc(consts_ready, 1)
            G.affine_select(out=dsel[:, :], in_=dsel[:, :], compare_op=ALU.not_equal, fill=1.0, base=-H,
                            pattern=[[0, P]], channel_multiplier=1).then_inc(consts_ready, 1)
            link.link(G.affine_select(out=tsel[:, :], in_=tsel[:, :], compare_op=ALU.is_ge, fill=0.0, base=0,
                                      pattern=[[-H, TPB]], channel_multiplier=1))
            G.affine_select(out=tsel[:, :], in_=tsel[:, :], compare_op=ALU.is_ge, fill=0.0, base=H - 1,
                            pattern=[[H, TPB]], channel_multiplier=-1).then_inc(consts_ready, 1)

            pool.wait_ge(tabs_complete, 1)

            def gather(b, i, par, peeled):
                pool.wait_ge(idx_ready, b + 1)
                pool.sem_inc(gathers_begun, 1)
                for g in range(NG):
                    if not peeled:
                        pool.wait_ge(vw_ready, NG * (b - 2) + g + 1)
                        pool.sem_inc(gathers_begun, 1)
                    for s in range(GRP):
                        t = g * GRP + s
                        G.indirect_dma_start(kv[:, par, t, :], None, kv_tab,
                                             bass.IndirectOffsetOnAxis(idxr[:, par, t:t + 1], 0))\
                         .then_inc(kv_land[par][g], 16)
            steps_by_pairs(pool, 0, NB, gather)

            pool.wait_ge(y_set, 1)
            G.tensor_tensor(xr[:, :, :], xr[:, :, :], lnw[:, 1:2, :].to_broadcast([P, NT, D]), ALU.add).then_inc(xb_ready, 1)
            for l in range(3):
                pool.wait_ge(tab_complete, l + 1)

                def gather_h(b, i, par, peeled):
                    B = b + NB * l
                    pool.wait_ge(src_ready, B + 1)
                    pool.sem_inc(gathers_begun, 1)
                    for g in range(NG):
                        if not (isinstance(B, int) and B == 0):
                            pool.wait_ge(sum_done, NG * (B - 1) + g + 1)
                            pool.sem_inc(gathers_begun, 1)
                        for s in range(GRP):
                            t = g * GRP + s
                            G.indirect_dma_start(gring[:, t, :], None, h_tab[l],
                                                 bass.IndirectOffsetOnAxis(idxr[:, par, t:t + 1], 0))\
                             .then_inc(row_land[g], 16)
                steps_by_pairs(pool, 0, NB, gather_h)

        @block.scalar
        def _(act):
            S = nc.scalar
            al = Links(act, act_link)
            for g in range(EG):
                n = min(P, ET - g * P)
                act.wait_ge(edge_turned, g + 1)
                S.activation(earr[:, :, g * P:g * P + n],
                             bank[g % 2][:, :].rearrange("p (k t) -> p k t", k=4)[:, :, 0:n], ACT.Copy)\
                 .then_inc(edge_cols, 1)
            act.wait_ge(weights_in, 16 * len(wloads))
            S.activation(sk[:, 1, :], sk[:, 0, :], ACT.Exp, scale=-1.0).then_inc(skip_exp, 1)

            def copy_xT(n, par):
                act.wait_ge(x_turned, n + 1)
                if not isinstance(n, int) or n >= 2:
                    act.wait_ge(qkv_done, n - 1)
                S.activation(xT[:, par, :, :], bank[par][:, :].rearrange("p (t f) -> p t f", t=T), ACT.Copy)\
                 .then_inc(xT_ready, 1)

            def copy_qkv(n, i, par):
                act.wait_ge(qkv_done, n + 1)
                if not isinstance(n, int) or n >= 2:
                    act.wait_ge(tab_kv, n - 1)
                    act.wait_ge(q_saved[par], 16 * i)
                S.activation(qkv[:, par, :, :], bank[2 + par][:, 0:3 * D].rearrange("p (k f) -> p k f", k=3), ACT.Copy)\
                 .then_inc(qkv_ready, 1)

            def copy_tab(n, i, par):
                act.wait_ge(tab_kv, n + 1)
                if not isinstance(n, int) or n >= 2:
                    act.wait_ge(tab_saved[par], 16 * i)
                S.activation(stage[:, par, GRP:R, :].rearrange("p r (k f) -> p k r f", k=2),
                             bank[6][:, :].rearrange("p (k r f) -> p k r f", k=2, r=R - GRP), ACT.Copy)\
                 .then_inc(kv_copied, 1)

            act.wait_ge(edge_cols, EG)
            copy_xT(0, 0)
            copy_xT(1, 1)
            copy_qkv(0, 0, 0)

            def table(n, i, par, peeled):
                copy_xT(n + 2, par)
                copy_qkv(n + 1, i + (par == 1), 1 - par)
                copy_tab(n, i, par)
            steps_by_pairs(act, 0, NT - 3, table)
            table(NT - 3, (NT - 3) // 2, (NT - 3) % 2, False)
            copy_qkv(NT - 1, (NT - 1) // 2, (NT - 1) % 2)
            copy_tab(NT - 2, (NT - 2) // 2, (NT - 2) % 2)
            copy_tab(NT - 1, (NT - 1) // 2, (NT - 1) % 2)

            def indices(b, par, peeled, n_land):
                if not peeled:
                    for g in range(NG):
                        act.wait_ge(kv_land[par][g], n_land)
                S.activation(idxr[:, par, :], idx_c[:, bass.ds(b * TPB, TPB)], ACT.Copy).then_inc(idx_ready, 1)

            def one_hot_T(b, i, par, g):
                if g == 0:
                    act.wait_ge(rel_in[par], 16 * (i + 1))
                if not (isinstance(b, int) and NG * b + g < 2):
                    act.wait_ge(q_done, NG * b + g - 1)
                al.link(S.activation(ohT[:, g % 2, :], relb[:, par, g * GRP * P:(g + 1) * GRP * P], ACT.Abs, scale=-1.0,
                                     bias=iota_p[:, 0:1]))
                S.activation(ohT[:, g % 2, :], ohT[:, g % 2, :], ACT.Relu, scale=-1.0, bias=epsc[:, 1:2]).then_inc(ohT_ready, 1)

            def one_hots(c, g):
                if not (isinstance(c, int) and c == 0):
                    act.wait_ge(agg_done, NG * (c - 1) + g + 1)
                for s in range(GRP):
                    al.inc(S.activation(oh[:, g, s, :], iota_j[:, :], ACT.Abs, scale=-1.0,
                                        bias=rel_c[:, bass.ds(c * TPB + (g * GRP + s), 1)]))
                al.wait()
                S.activation(oh[:, g, :, :], oh[:, g, :, :], ACT.Relu, scale=-1.0, bias=epsc[:, 1:2]).then_inc(oh_ready, 1)

            def weights(c):
                if not (isinstance(c, int) and c == 0):
                    act.wait_ge(agg_done, NG * c)
                S.activation(exw[:, :, H], ew_c[:, bass.ds(c * TPB, TPB)], ACT.Copy).then_inc(ewcol_ready, 1)
                act.wait_ge(f_diff, c + 1)
                if not (isinstance(c, int) and c == 0):
                    act.wait_ge(scaled, c)
                S.activation(f9[0:H, :], fd[:, :], ACT.Exp).then_inc(f_ready, 1)
                act.wait_ge(dif_ready, c + 1)
                if not (isinstance(c, int) and c == 0):
                    act.wait_ge(ex_turned, c)
                S.activation(exT[:, :], dif[:, :], ACT.Exp).then_inc(exT_ready, 1)
                act.wait_ge(ex_turned, c + 1)
                S.activation(exw[:, :, 0:H], bank[2][:, P:2 * P].rearrange("p (t h) -> p t h", h=H), ACT.Copy)\
                 .then_inc(exw_ready, 1)

            act.wait_ge(consts_ready, 7)
            act.wait_ge(exw_zero, 1)
            indices(0, 0, True, 0)

            def attend(b, i, par, peeled):
                al.at((TPB + NG) * (b - 1) + NG + 2)
                if not (isinstance(b, int) and b == NB - 1):
                    indices(b + 1, 1 - par, False, 64 * (i + par))
                one_hot_T(b, i, par, 2)
                one_hot_T(b, i, par, 3)
                for g in range(NG):
                    one_hots(b - 1, g)
                weights(b - 1)
                if not (isinstance(b, int) and b == NB - 1):
                    one_hot_T(b + 1, i + par, 1 - par, 0)
                    one_hot_T(b + 1, i + par, 1 - par, 1)
            indices(1, 1, True, 0)
            al.at(0)
            for g in range(NG):
                one_hot_T(0, 0, 0, g)
            for g in range(2):
                one_hot_T(1, 0, 1, g)
            steps_by_pairs(act, 1, NB, attend, tail=2)
            al.at((TPB + NG) * (NB - 1) + NG)
            for g in range(NG):
                one_hots(NB - 1, g)
            weights(NB - 1)

            def root(n, w):
                act.wait_ge(var_ready, n)
                S.activation(rs[:, 0:w], mv[:, 0:w, 1], ACT.Sqrt, bias=epsc[:, 0:1]).then_inc(std_ready, 1)

            act.wait_ge(deg_ready, 1)
            S.activation(nodec[:, :, H], nodec[:, :, H], ACT.Sqrt).then_inc(root_ready, 1)
            act.wait_ge(deg_ready, 3)
            S.activation(big[:, 0:NP_].rearrange("p (n h d) -> p n h d", h=H, d=DH),
                         nodec[:, :, 0:H].rearrange("p n (h a) -> p n h a", a=1).to_broadcast([P, NT, H, DH]), ACT.Copy)\
             .then_inc(den_wide, 1)
            root(1, NT)

            def normalize(k):
                act.wait_ge(shift_ready, k)
                for n in range(NT):
                    if k == 2:
                        o_ = xr[:, n, :]
                    else:
                        o_ = big[:, n * D:(n + 1) * D]
                    S.activation(o_, big[:, n * D:(n + 1) * D], ACT.Identity, bias=shf[:, n:n + 1], scale=rs[:, n:n + 1])\
                     .then_inc(y_normed if k == 1 else x1_ready, 1)
            normalize(1)
            root(2, NT)
            normalize(2)
            def rows_out(l, c):
                c0, cw = CH[c]
                n, a, tiles = NCH * l + c, (NCH * l + c) % 2, cw // P
                act.wait_ge(rows_turned, n + 1)
                if n >= 2:
                    act.wait_ge(rows_saved[a], 16 * (n // 2))
                S.activation(xT[:, a, 0:tiles, :], bank[4 + n % 2][:, 0:cw].rearrange("p (t f) -> p t f", f=D),
                             ACT.Copy).then_inc(rows_ready, 1)

            for c in range(NCH):
                rows_out(0, c)
            for l in range(3):

                def sources(b, i, par, peeled):
                    B = b + NB * l
                    if not (isinstance(B, int) and B < 2):
                        for g in range(NG):
                            act.wait_ge(row_land[g], 64 * (B - 1))
                    S.activation(idxr[:, par, :], src_c[:, bass.ds(b * TPB, TPB)], ACT.Copy).then_inc(src_ready, 1)
                if l == 0:
                    for a in range(2):
                        for g in range(NG):
                            act.wait_ge(kv_land[a][g], 64 * (NB // 2))
                steps_by_pairs(act, 0, NB, sources)
                for c, (c0, cw) in enumerate(CH):
                    act.wait_ge(h_scaled, NCH * l + c + 1)
                    S.activation(hd[:, c0:c0 + cw], hd[:, c0:c0 + cw], ACT.Identity, bias=gcnv[:, l:l + 1])\
                     .then_inc(h_ready, 1)
                root(3 + l, 1)
                act.wait_ge(bn_ready, l + 1)
                for c, (c0, cw) in enumerate(CH):
                    S.activation(hd[:, c0:c0 + cw], hd[:, c0:c0 + cw], ACT.Relu if l < 2 else ACT.Identity,
                                 bias=bn[:, 1:2], scale=bn[:, 0:1]).then_inc(act_ready, 1)
                    if l < 2 and c >= 2:
                        rows_out(l + 1, c - 2)
                if l < 2:
                    rows_out(l + 1, NCH - 2)
                    rows_out(l + 1, NCH - 1)
            root(6, NT)

        @block.tensor
        def _(pe):
            M = nc.tensor
            pe.wait_ge(consts_ready, 7)
            for g in range(EG):
                n = min(P, ET - g * P)
                pe.wait_ge(edge_rows, g + 1)
                if g >= 2:
                    pe.wait_ge(edge_cols, g - 1)
                for k, a in enumerate((ro[0:n, g % 2, 0, :], ro[0:n, g % 2, 1, :], ef[0:n, g % 2, 3, :], ewi[0:n, g, :])):
                    last = M.transpose(bank[g % 2][:, k * P:k * P + n], a, ident[0:n, 0:n])
                last.then_inc(edge_turned, 1)
            M.transpose(bank[2][:, 0:H], hselT[:, :], ident[0:H, 0:H]).then_inc(hsel_turned, 1)
            pe.wait_ge(nt_ready, 1)
            M.transpose(bank[3][:, 0:NT], ntf[:, :], ident[0:NT, 0:NT]).then_inc(nt_turned, 1)
            pe.wait_ge(weights_in, 16 * len(wloads))
            pe.wait_ge(edge_cols, EG)
            pe.wait_ge(masks_ready, 1)
            pe.wait_ge(hsel_ready, 1)

            def turn(n, par):
                pe.wait_ge(xm_ready, n + 1)
                if not isinstance(n, int) or n >= 2:
                    pe.wait_ge(xT_ready, n - 1)
                for t in range(T):
                    last = M.transpose(bank[par][:, t * D:(t + 1) * D], xm[:, par, t, :], ident[:, :])
                last.then_inc(x_turned, 1)

            def project(n, par):
                pe.wait_ge(xT_ready, n + 1)
                if not isinstance(n, int) or n >= 2:
                    pe.wait_ge(qkv_ready, n - 1)
                o_ = bank[2 + par]
                for t in range(T):
                    M.matmul(o_[:, 0:D], xT[:, par, t, :], wkqv[:, 0, t, :], start=t == 0, stop=t == T - 1)
                for k in (1, 2):
                    for t in range(T):
                        last = M.matmul(o_[:, k * D:(k + 1) * D], wkqv[:, k, t, :], xT[:, par, t, :],
                                        start=t == 0, stop=t == T - 1)
                last.then_inc(qkv_done, 1)

            def relate(n, par):
                pe.wait_ge(qkv_ready, n + 1)
                first = isinstance(n, int) and n == 0
                for k, (o_, done, copied) in enumerate(((bank[4], tab_k, k_copied), (bank[5], tab_v, v_copied))):
                    if not first:
                        pe.wait_ge(copied, n)
                    M.matmul(o_[:, :], qkv[:, par, 1 + k, :], bd[:, k, 0:GRP, :].rearrange("p r f -> p (r f)"),
                             start=True, stop=True).then_inc(done, 1)
                if not first:
                    pe.wait_ge(kv_copied, n)
                w = (R - GRP) * D
                for k in range(2):
                    last = M.matmul(bank[6][:, k * w:(k + 1) * w], qkv[:, par, 1 + k, :],
                                    bd[:, k, GRP:R, :].rearrange("p r f -> p (r f)"), start=True, stop=True)
                last.then_inc(tab_kv, 1)

            turn(0, 0)
            turn(1, 1)
            project(0, 0)

            def table(n, i, par, peeled):
                turn(n + 2, par)
                project(n + 1, 1 - par)
                relate(n, par)
            steps_by_pairs(pe, 0, NT - 3, table)
            table(NT - 3, 0, (NT - 3) % 2, False)
            project(NT - 1, (NT - 1) % 2)
            relate(NT - 2, (NT - 2) % 2)
            relate(NT - 1, (NT - 1) % 2)
            pe.wait_ge(k_copied, NT)
            pe.wait_ge(v_copied, NT)
            pe.wait_ge(kv_copied, NT)
            pe.wait_ge(qkv_ready, NT)

            def q_rows(b, i, g):
                pe.wait_ge(ohT_ready, NG * b + g + 1)
                pe.wait_ge(qwin_in[g], 64 * (b + 1))
                if not (isinstance(b, int) and NG * b + g < 2):
                    pe.wait_ge(logit_done, NG * b + g - 1)
                for s in range(GRP):
                    last = M.matmul(bank[g % 2][:, s * D:(s + 1) * D], ohT[:, g % 2, s * P:(s + 1) * P],
                                    qwin[:, g * GRP + s, :], start=True, stop=True)
                last.then_inc(q_done, 1)

            def aggregate(c, g):
                pe.wait_ge(oh_ready, NG * c + g + 1)
                if g == 0:
                    pe.wait_ge(exw_ready, c + 1)
                    pe.wait_ge(ewcol_ready, c + 1)
                if not (isinstance(c, int) and NG * c + g < 2):
                    pe.wait_ge(acc_added, TPB * c + GRP * (g - 1))
                o_ = [bank[4 + 2 * (g % 2) + s // 2][:, (s % 2) * 2 * P:(s % 2 + 1) * 2 * P] for s in range(GRP)]
                for s in range(GRP):
                    M.matmul(o_[s][:, P:2 * P], exw[:, g * GRP + s, :], oh[:, g, s, :], start=True, stop=True)
                pe.wait_ge(vw_ready, NG * c + g + 1)
                for s in range(GRP):
                    last = M.matmul(o_[s][:, 0:P], vw[:, g * GRP + s, :], oh[:, g, s, :], start=True, stop=True)
                last.then_inc(agg_done, 1)

            def chain_f(c):
                pe.wait_ge(fwd_ends, c + 1)
                pe.wait_ge(flags_ready, 2 * (c + 1))
                M.matmul(bank[3][0:H, 0:2 * TPB], hsel[:, :], rhs[:, 0, :], start=True, stop=True).then_inc(fwd_chained, 1)

            def spread_f(c, par_c):
                pe.wait_ge(fwd_carry, c + 1)
                M.matmul(bank[3][:, 64:64 + TPB], hselT[:, :], sx[:, par_c, 0:TPB], start=True, stop=True).then_inc(fwd_spread, 1)

            def chain_b(c):
                pe.wait_ge(bwd_ends, c + 1)
                M.matmul(bank[3][0:H, 128:128 + 2 * TPB], hsel[:, :], rhs[:, 1, :], start=True, stop=True).then_inc(bwd_chained, 1)

            def spread_b(c):
                pe.wait_ge(bwd_carry, c + 1)
                M.matmul(bank[3][:, 192:192 + TPB], hselT[:, :], sr[:, 1:TPB + 1], start=True, stop=True).then_inc(bwd_spread, 1)

            def turn_ex(c):
                pe.wait_ge(exT_ready, c + 1)
                pe.wait_ge(f_ready, c + 1)
                M.matmul(bank[2][:, 2 * P:2 * P + 1], fsel[0:H, :], f9[0:H, :], start=True, stop=True)
                M.matmul(bank[2][:, 2 * P + 1:2 * P + 2], ident[0:H + 1, :], f9[:, :], start=True, stop=True).then_inc(f_spread, 1)
                M.transpose(bank[2][:, P:2 * P], exT[:, :], ident[:, :]).then_inc(ex_turned, 1)

            def turn_logit(b):
                pe.wait_ge(logit_done, NG * (b + 1))
                if not (isinstance(b, int) and b == 0):
                    pe.wait_ge(dif_ready, b)
                    pe.wait_ge(exw_ready, b)
                    pe.wait_ge(scaled, b)
                M.transpose(bank[2][:, 0:P], logit[:, :], ident[:, :]).then_inc(logit_turned, 1)

            def attend(b, i, par, peeled):
                c = b - 1
                if isinstance(b, int) and b == 0:
                    for g in range(NG):
                        q_rows(b, i, g)
                    turn_logit(b)
                    q_rows(b + 1, 0, 0)
                    q_rows(b + 1, 0, 1)
                    return
                chain_f(c)
                if not (isinstance(b, int) and b == 1):
                    aggregate(c - 1, NG - 1)
                q_rows(b, i, 2)
                spread_f(c, 1 - par)
                q_rows(b, i, 3)
                chain_b(c)
                spread_b(c)
                turn_ex(c)
                aggregate(c, 0)
                aggregate(c, 1)
                turn_logit(b)
                if not (isinstance(b, int) and b == NB - 1):
                    q_rows(b + 1, i + par, 0)
                    q_rows(b + 1, i + par, 1)
                aggregate(c, 2)
            steps_by_pairs(pe, 0, NB, attend, tail=2)
            c = NB - 1
            chain_f(c)
            aggregate(c - 1, NG - 1)
            spread_f(c, 1)
            chain_b(c)
            spread_b(c)
            turn_ex(c)
            for g in range(NG):
                aggregate(c, g)

            pe.wait_ge(acc_added, ET)
            for n in range(NT):
                last = M.transpose(bank[0][:, n * (H + 1):(n + 1) * (H + 1)], hd[0:H + 1, n * P:(n + 1) * P],
                                   ident[0:H + 1, 0:H + 1])
            last.then_inc(den_turned, 1)
            pe.wait_ge(den_wide, 1)
            for c, (c0, cw) in enumerate(CH):
                if c >= 3:
                    pe.wait_ge(attn_scaled, c - 2)
                for t in range(cw // P):
                    last = M.transpose(bank[1 + c % 3][:, t * P:(t + 1) * P],
                                       big[:, c0 + t * P:c0 + (t + 1) * P],
                                       ident[:, :])
                last.then_inc(den_spread, 1)
            for n in range(NT):
                pe.wait_ge(attn_scaled, NCH)
                if n >= 2:
                    pe.wait_ge(y_sum, 8 * (n // 2 - 1) + 6 + n % 2 + 1)
                M.matmul(bank[4 + n % 2][:, :], acc[:, n * P:(n + 1) * P], wa[:, :, :].rearrange("p t f -> p (t f)"),
                         start=True, stop=True).then_inc(types_done, 1)
            pe.wait_ge(x1_ready, NT)
            for c, (c0, cw) in enumerate(CH):
                if c >= 2:
                    pe.wait_ge(acc_set, c - 1)
                for t in range(cw // P):
                    M.transpose(bank[c % 2][:, t * P:(t + 1) * P],
                                nodec[:, c0 // P + t, H:H + 1].to_broadcast([P, P]), ident[:, :])
                for t in range(cw // P):
                    last = M.transpose(bank[2 + c % 2][:, t * P:(t + 1) * P], xr[:, c0 // P + t, :], ident[:, :])
                last.then_inc(x1_turned, 1)
            for l in range(3):
                for c, (c0, cw) in enumerate(CH):
                    n = NCH * l + c
                    pe.wait_ge(acc_set, n + 1)
                    if n >= 2:
                        pe.wait_ge(rows_ready, n - 1)
                    for t in range(cw // P):
                        last = M.transpose(bank[4 + n % 2][:, t * P:(t + 1) * P], acc[:, c0 + t * P:c0 + (t + 1) * P],
                                           ident[:, :])
                    last.then_inc(rows_turned, 1)

                def sums(b, i, par, peeled):
                    B = b + NB * l
                    for g in range(NG):
                        pe.wait_ge(row_land[g], 64 * (B + 1))
                        pe.wait_ge(wt_ready, TPB * B + GRP * (g + 1))
                        if not (isinstance(B, int) and B == 0):
                            pe.wait_ge(win_added, TPB * (B - 1) + GRP * (g + 1))
                        for s in range(GRP):
                            last = M.matmul(bank[g][:, s * P:(s + 1) * P], gring[:, g * GRP + s, :], oh[:, g, s, :],
                                            start=True, stop=True)
                        last.then_inc(sum_done, 1)
                steps_by_pairs(pe, 0, NB, sums)
                pe.wait_ge(win_added, ET * (l + 1))
                for c, (c0, cw) in enumerate(CH):
                    if c >= 4:
                        pe.wait_ge(h_scaled, NCH * l + c - 3)
                    M.matmul(bank[c % 4][:, 0:cw], wg[:, l, :], acc[:, c0:c0 + cw], start=True, stop=True)\
                     .then_inc(lin_done, 1)
            for c, (c0, cw) in enumerate(CH):
                pe.wait_ge(act_ready, NCH * 2 + c + 1)
                if c >= 4:
                    pe.wait_ge(res_added, c - 3)
                for t in range(cw // P):
                    last = M.transpose(bank[4 + c % 4][:, t * P:(t + 1) * P], hd[:, c0 + t * P:c0 + (t + 1) * P],
                                       ident[:, :])
                last.then_inc(h_turned, 1)

        @block.vector
        def _(dve):
            V = nc.vector
            dl = Links(dve, dve_link)

            V.memset(ei[:, GF, 0:3, :], PAD_DST).then_inc(pads_set, 1)
            V.memset(ei[:, GF, 3:5, :], 0).then_inc(pads_set, 1)
            V.memset(ei[0:1, 0, 1, 0:1], -5).then_inc(pads_set, 1)
            V.memset(ewi[:, GF, :], 0.0).then_inc(pads_set, 1)
            V.memset(nti[:, :], 0).then_inc(pads_set, 1)
            V.memset(base_row[:, :], 0).then_inc(pads_set, 1)
            V.memset(bd[:, :, :, :], 0.0).then_inc(pads_set, 1)
            V.memset(xr[:, NF, :], 0.0).then_inc(pads_set, 1)
            V.memset(epsc[:, 0:1], EPS).then_inc(pads_set, 1)
            V.memset(epsc[:, 1:2], 1.0).then_inc(pads_set, 1)
            V.memset(f9[:, :], 1.0).then_inc(pads_set, 1)

            dve.wait_ge(edges_in, 16 * len(loads))
            for g in range(EG):
                n, a = min(P, ET - g * P), g % 2
                if g >= 2:
                    dve.wait_ge(edge_turned, g - 1)
                    dve.wait_ge(edge_saved[a], 48 * (g // 2))
                e_ = ef[0:n, a, :, :]
                dl.inc(V.tensor_copy(e_[:, 0:4, :], ei[0:n, g, 0:4, :]))
                dl.link(V.tensor_copy(ro[0:n, a, 2, :], ei[0:n, g, 4, :]))
                dl.inc(V.tensor_tensor(nb[0:n, a, 0, :], e_[:, 0, :], e_[:, 1, :], ALU.is_equal))
                dl.inc(V.tensor_tensor(nb[0:n, a, 1, :], e_[:, 0, :], e_[:, 2, :], ALU.is_equal))
                dl.inc(V.tensor_scalar(ro[0:n, a, 3, 0:1], e_[:, 0, 0:1], float(PAD_DST) - 1.0, e_[:, 0, 0:1],
                                       ALU.is_lt, ALU.mult))
                dl.link(V.scalar_tensor_tensor(out=ro[0:n, a, 1, :], in0=e_[:, 3, :], scalar=float(R),
                                               in1=ro[0:n, a, 2, :], op0=ALU.mult, op1=ALU.add))
                dl.inc(V.tensor_scalar(nb[0:n, a, 0:2, :], nb[0:n, a, 0:2, :], 1.0, BIG, ALU.subtract, ALU.mult))
                dl.inc(V.tensor_scalar(relw[0:n, a, :], e_[:, 0, :], ro[0:n, a, 3, 0:1], None, ALU.subtract))
                dl.wait(1)
                V.tensor_scalar(ro[0:n, a, 0, :], e_[:, 0, :], ro[0:n, a, 3, 0:1], None, ALU.subtract).then_inc(edge_rows, 1)
                dl.wait()
            dve.wait_ge(weights_in, 16 * len(wloads))
            V.tensor_copy(ntf[:, :], nti[:, :]).then_inc(nt_ready, 1)
            dve.wait_ge(skip_exp, 1)
            dl.link(V.tensor_scalar(sk[:, 1, :], sk[:, 1, :], 1.0, None, ALU.add))
            dl.link(V.reciprocal(sk[:, 2, :], sk[:, 1, :]))
            dl.link(V.tensor_scalar(pri[:, :], pri[:, :], float(DH) ** -0.5, None, ALU.mult))
            for r in range(R):
                dl.inc(V.tensor_scalar(bd[:, 0, r, :], bd[:, 0, r, :], pri[:, r:r + 1], None, ALU.mult))
            dve.wait_ge(hsel_turned, 1)
            V.tensor_copy(hsel[:, :], bank[2][:, 0:H]).then_inc(hsel_ready, 1)
            dve.wait_ge(nt_turned, 1)
            dl.link(V.tensor_copy(nt_c[:, :], bank[3][:, 0:NT]))
            for t in range(T):
                dl.inc(V.tensor_scalar(tmask[:, :, t], nt_c[:, :], float(t), None, ALU.is_equal))
            dl.wait()
            dl.link(V.tensor_tensor(gmask[:, :, :], tmask[:, :, :], sk[:, 2:3, :].to_broadcast([P, NT, T]), ALU.mult))
            dl.link(V.tensor_reduce(keep[:, :], gmask[:, :, :], AX.X, ALU.add))
            dl.link(V.tensor_scalar(keep[:, :], keep[:, :], -1.0, 2.0, ALU.mult, ALU.add))
            dl.link(V.memset(sx[:, :, :], -BIG))
            dl.link(V.memset(sr[:, :], -BIG))
            V.memset(acc[:, :], 0.0).then_inc(masks_ready, 1)
            dl.inc(V.memset(hd[:, :], 0.0))
            dve.wait_ge(edge_turned, EG)
            dve.wait_ge(edge_saved[0], 48 * ((EG + 1) // 2))
            dve.wait_ge(edge_saved[1], 48 * (EG // 2))
            V.memset(oh[:, 0, 0, :], 0.0).then_inc(masks_ready, 1)
            dl.wait()
            prep_links = dl.n

            def mask_x(n, par):
                if not isinstance(n, int) or n >= 2:
                    dve.wait_ge(x_turned, n - 1)
                V.tensor_tensor(xm[:, par, :, :], xr[:, bass.ds(n, 1), :].to_broadcast([P, T, D]),
                                tmask[:, bass.ds(n, 1), :].rearrange("p a t -> p t a").to_broadcast([P, T, D]), ALU.mult)\
                 .then_inc(xm_ready, 1)

            def copy_tab(n, i, par):
                if not isinstance(n, int) or n >= 2:
                    dve.wait_ge(tab_saved[par], 16 * i)
                for k, (done, copied) in enumerate(((tab_k, k_copied), (tab_v, v_copied))):
                    dve.wait_ge(done, n + 1)
                    V.tensor_copy(stage[:, par, 0:GRP, k * D:(k + 1) * D],
                                  bank[4 + k][:, :].rearrange("p (r f) -> p r f", r=GRP)).then_inc(copied, 1)

            dve.wait_ge(x_in, 32)
            mask_x(0, 0)
            mask_x(1, 1)

            def table(n, i, par, peeled):
                mask_x(n + 2, par)
                copy_tab(n, i, par)
            steps_by_pairs(dve, 0, NT - 3, table)
            table(NT - 3, (NT - 3) // 2, (NT - 3) % 2, False)
            for n in (NT - 2, NT - 1):
                copy_tab(n, n // 2, n % 2)

            dve.wait_ge(tabs_complete, 1)
            V.memset(exw[:, :, :], 0.0).then_inc(exw_zero, 1)

            def products(b, i, par, g):
                dve.wait_ge(kv_land[par][g], 64 * (i + 1))
                dve.wait_ge(q_done, NG * b + g + 1)
                kg = kv[:, par, g * GRP:(g + 1) * GRP, 0:D]
                dl.inc(V.tensor_tensor(kg, kg, bank[g % 2][:, :].rearrange("p (s f) -> p s f", s=GRP), ALU.mult))

            def logits(b, par, g):
                dl.wait()
                if g == 0 and not (isinstance(b, int) and b == 0):
                    dve.wait_ge(logit_turned, b)
                V.tensor_reduce(logit[:, g * GRP * H:(g + 1) * GRP * H].rearrange("p (s h) -> p s h", h=H),
                                kv[:, par, g * GRP:(g + 1) * GRP, 0:D].rearrange("p s (h d) -> p s h d", d=DH),
                                AX.X, ALU.add).then_inc(logit_done, 1)

            def flags(c, i, pc):
                dve.wait_ge(neg_in[pc], 32 * (i + 1))
                if not (isinstance(c, int) and c == 0):
                    dve.wait_ge(bwd_chained, c)
                dl.link(V.tensor_reduce(ini[:, 2:4], negs[:, pc, :, :], AX.X, ALU.min))
                for k in range(2):
                    V.tensor_scalar(rhs[:, k, TPB:2 * TPB], tsel[:, :], ini[:, 2 + k:3 + k], None, ALU.mult)\
                     .then_inc(flags_ready, 1)

            def ends(run, k, at, signal):
                V.tensor_scalar(rhs[:, k, 0:TPB], tsel[:, :], run[:, at:at + 1], None, ALU.mult).then_inc(signal, 1)

            def max_1(c, pc):
                dve.wait_ge(logit_turned, c + 1)
                if not (isinstance(c, int) and c == 0):
                    dve.wait_ge(ex_turned, c)
                    dve.wait_ge(dif_ready, c)
                dl.inc(V.tensor_tensor_scan(mxf[:, :], negs[:, pc, 0, :], bank[2][:, 0:P], -BIG, ALU.add, ALU.max))

            def max_2(c, pc):
                dve.wait_ge(fwd_chained, c + 1)
                dl.link(V.tensor_copy(negall[:, 0, :], bank[3][0:H, TPB:2 * TPB]))
                V.tensor_tensor_scan(sx[:, pc, 1:TPB + 1], negall[:, 0, :], bank[3][0:H, 0:TPB], sx[:, pc, 0:1],
                                     ALU.add, ALU.max).then_inc(fwd_carry, 1)

            def initial(c, col, k):
                dl.link(V.tensor_tensor(tmp16[:, :], bank[3][:, col:col + TPB], tsel[:, :], ALU.mult))
                dl.link(V.tensor_reduce(ini[:, k:k + 1], tmp16[:, :], AX.X, ALU.add))

            def max_3(c, pc):
                dve.wait_ge(fwd_spread, c + 1)
                initial(c, 64, 0)
                dl.link(V.tensor_tensor_scan(mxf[:, :], negs[:, pc, 0, :], bank[2][:, 0:P], ini[:, 0:1], ALU.add, ALU.max))
                dl.link(V.tensor_tensor_scan(mxb[:, ::-1], negs[:, pc, 1, ::-1], mxf[:, ::-1], -BIG, ALU.add, ALU.max))
                ends(mxb, 1, 0, bwd_ends)

            def max_4(c, pc):
                dve.wait_ge(bwd_chained, c + 1)
                dve.wait_ge(fwd_carry, c + 1)
                dl.inc(V.tensor_copy(sx[:, 1 - pc, 0:1], sx[:, pc, TPB:TPB + 1]))
                dl.link(V.tensor_copy(negall[:, 1, :], bank[3][0:H, 128 + TPB:128 + 2 * TPB]))
                V.tensor_tensor_scan(sr[:, TPB - 1::-1], negall[:, 1, ::-1], bank[3][0:H, 128 + TPB - 1:127:-1], -BIG,
                                     ALU.add, ALU.max).then_inc(bwd_carry, 1)
                dve.wait_ge(bwd_carry, c + 1)
                dl.link(V.tensor_tensor(fd[:, :], sx[:, pc, 0:1], sr[:, 0:1], ALU.subtract))
                V.tensor_scalar(fd[:, :], fd[:, :], 0.0, None, ALU.min).then_inc(f_diff, 1)

            def max_5(c, pc):
                dve.wait_ge(bwd_spread, c + 1)
                initial(c, 192, 1)
                dl.link(V.tensor_tensor_scan(mxb[:, ::-1], negs[:, pc, 1, ::-1], mxf[:, ::-1], ini[:, 1:2], ALU.add, ALU.max))
                if not (isinstance(c, int) and c == 0):
                    dve.wait_ge(exT_ready, c)
                V.tensor_tensor(dif[:, :], bank[2][:, 0:P], mxb[:, :], ALU.subtract).then_inc(dif_ready, 1)

            def weigh(c, pc, g):
                if g == 0:
                    dve.wait_ge(exw_ready, c + 1)
                if not (isinstance(c, int) and c == 0):
                    dve.wait_ge(agg_done, NG * (c - 1) + g + 1)
                V.tensor_tensor(vw[:, g * GRP:(g + 1) * GRP, :].rearrange("p s (h d) -> p s h d", d=DH),
                                kv[:, pc, g * GRP:(g + 1) * GRP, D:2 * D].rearrange("p s (h d) -> p s h d", d=DH), exw[:, g * GRP:(g + 1) * GRP, 0:H].rearrange("p s (h a) -> p s h a", a=1)
                                .to_broadcast([P, GRP, H, DH]), ALU.mult).then_inc(vw_ready, 1)

            def scale_open(c, firsts):
                dve.wait_ge(f_spread, c + 1)
                a_ = sums2[:, :, bass.ds(firsts[0], 1)]
                if not (isinstance(c, int) and c == 0):
                    dve.wait_ge(acc_added, TPB * c)
                V.tensor_tensor(a_, a_, bank[2][:, 2 * P:2 * P + 2].rearrange("p (k a) -> p k a", a=1), ALU.mult)\
                 .then_inc(scaled, 1)
                dve.wait_ge(scaled, c + 1)

            def add_window(c, g, s, firsts):
                t = g * GRP + s
                if s == 0:
                    dve.wait_ge(agg_done, NG * c + g + 1)
                if not (isinstance(c, int) and c == 0 and t == 0):
                    dve.wait_ge(acc_added, TPB * c + t)
                w_ = sums2[:, :, bass.ds(firsts[s], P)]
                d_ = bank[4 + 2 * (g % 2) + s // 2][:, (s % 2) * 2 * P:(s % 2 + 1) * 2 * P]
                V.tensor_tensor(w_, w_, d_.rearrange("p (k j) -> p k j", k=2), ALU.add).then_inc(acc_added, 1)

            def starts(c, g):
                return load_starts(mybir.EngineType.DVE, c * TPB + g * GRP)

            def find_max(b, i, par, f):
                c, pc = b - 1, 1 - par
                final = isinstance(b, int) and b == NB

                def late(g, s):
                    if f:
                        add_window(c - 1, g, s, f[g])
                late(1, 0)
                max_1(c, pc)
                late(1, 1)
                dl.wait()
                ends(mxf, 0, P - 1, fwd_ends)
                late(1, 2)
                if not final:
                    products(b, i, par, 0)
                late(1, 3)
                if not final:
                    logits(b, par, 0)
                max_2(c, pc)
                late(2, 0)
                if not final:
                    products(b, i, par, 1)
                late(2, 1)
                if not final:
                    logits(b, par, 1)
                max_3(c, pc)
                late(2, 2)
                if not final:
                    products(b, i, par, 2)
                    logits(b, par, 2)
                max_4(c, pc)
                late(2, 3)
                max_5(c, pc)
                for s in range(GRP):
                    late(3, s)

            def weigh_batch(c, pc, i):
                weigh(c, pc, 0)
                weigh(c, pc, 1)
                f = [starts(c, g) for g in (0, 1)]
                if not (isinstance(c, int) and c == NB - 1):
                    flags(c + 1, i, 1 - pc)
                weigh(c, pc, 2)
                weigh(c, pc, 3)
                f += [starts(c, g) for g in (2, 3)]
                scale_open(c, f[0])
                if not (isinstance(c, int) and c == NB - 1):
                    products(c + 1, i, 1 - pc, NG - 1)
                    logits(c + 1, 1 - pc, NG - 1)
                for s in range(GRP):
                    add_window(c, 0, s, f[0])
                return f

            def step(b, i, par, peeled):
                dl.at(counts["links"] + counts.get("step", 0) * (b - 1))
                f = weigh_batch(b - 1, 1 - par, i)
                find_max(b + 1, i + par, 1 - par, f)
                if not (isinstance(b, int) and b == NB - 1):
                    assert counts.setdefault("step", dl.n) == dl.n
            counts = {}
            dl.at(prep_links)
            for g in range(NG):
                products(0, 0, 0, g)
                logits(0, 0, g)
            flags(0, 0, 0)
            find_max(1, 0, 1, None)
            counts["links"] = prep_links + dl.n
            steps_by_pairs(dve, 1, NB, step, tail=2)
            f = weigh_batch(NB - 1, 1, None)
            for g in (1, 2, 3):
                for s in range(GRP):
                    add_window(NB - 1, g, s, f[g])
            dl.at(dl.base + dl.n)
            yr = big[:, 0:NP_].rearrange("p (n f) -> p n f", f=D)

            dve.wait_ge(den_turned, 1)
            dl.link(V.tensor_scalar(nodec[:, :, 0:H], bank[0][:, 0:NT * (H + 1)].rearrange("p (n h) -> p n h", h=H + 1)[:, :, 0:H],
                                    1e-9, None, ALU.max))
            V.tensor_scalar(nodec[:, :, H], bank[0][:, 0:NT * (H + 1)].rearrange("p (n h) -> p n h", h=H + 1)[:, :, H],
                            1.0, 1e-30, ALU.add, ALU.max).then_inc(deg_ready, 1)
            dve.wait_ge(root_ready, 1)
            V.reciprocal(nodec[:, :, :], nodec[:, :, :]).then_inc(deg_ready, 1)
            dve.wait_ge(deg_ready, 2)
            V.scalar_tensor_tensor(out=nodec[:, :, H], in0=nodec[:, :, H], scalar=5e14, in1=nodec[:, :, H],
                                   op0=ALU.is_lt, op1=ALU.mult).then_inc(deg_ready, 1)
            for c, (c0, cw) in enumerate(CH):
                dve.wait_ge(den_spread, c + 1)
                if c == 0:
                    dve.wait_ge(acc_added, ET)
                V.tensor_tensor(acc[:, c0:c0 + cw], acc[:, c0:c0 + cw], bank[1 + c % 3][:, 0:cw], ALU.mult).then_inc(attn_scaled, 1)
            V.tensor_tensor(yr, xr[:, :, :], keep[:, :].rearrange("p (n a) -> p n a", a=1).to_broadcast([P, NT, D]),
                            ALU.mult).then_inc(y_set, 1)
            dve.wait_ge(y_set, 1)

            def y_rows(i, tiles):
                dve.wait_ge(types_done, 2 * i + len(tiles))
                per = len(tiles)
                for t in range(T):
                    for k in tiles:
                        if t:
                            dve.wait_ge(y_sum, 8 * i + per * (t - 1) + k + 1)
                        y_ = big[:, bass.ds((2 * i + k) * D, D)]
                        V.scalar_tensor_tensor(out=y_, in0=bank[4 + k][:, t * D:(t + 1) * D],
                                               scalar=gmask[:, bass.ds(2 * i + k, 1), t:t + 1].rearrange("p a t -> p (a t)"),
                                               in1=y_, op0=ALU.mult, op1=ALU.add).then_inc(y_sum, 1)
                for k in tiles:
                    dve.wait_ge(y_sum, 8 * i + per * (T - 1) + k + 1)
                    V.bn_stats(bst[:, bass.ds(2 * i + k, 1), :].rearrange("p a s -> p (a s)"), big[:, bass.ds((2 * i + k) * D, D)])\
                     .then_inc(stat_done, 1)
            with dve.Fori(0, NT // 2) as i:
                y_rows(i, (0, 1))
            y_rows(NT // 2, (0,))

            def row_moments(k):
                dve.wait_ge(stat_done, NT * k)
                dl.inc(V.tensor_tensor(mv[:, :, 0], bst[:, :, 1], bst[:, :, 4], ALU.add))
                dl.inc(V.tensor_tensor(mv[:, :, 1], bst[:, :, 1], bst[:, :, 4], ALU.subtract))
                dl.link(V.tensor_tensor(bst[:, :, 0], bst[:, :, 2], bst[:, :, 5], ALU.add))
                dl.inc(V.tensor_scalar(mv[:, :, 0], mv[:, :, 0], 0.5, None, ALU.mult))
                dl.inc(V.tensor_scalar(bst[:, :, 0], bst[:, :, 0], 1.0 / D, None, ALU.mult))
                dl.link(V.scalar_tensor_tensor(out=mv[:, :, 1], in0=mv[:, :, 1], scalar=0.25, in1=mv[:, :, 1],
                                               op0=ALU.mult, op1=ALU.mult))
                V.tensor_tensor(mv[:, :, 1], mv[:, :, 1], bst[:, :, 0], ALU.add).then_inc(var_ready, 1)
                dve.wait_ge(std_ready, {1: 1, 2: 2, 3: 6}[k])
                dl.link(V.reciprocal(rs[:, :], rs[:, :]))

            def negated_shift(k):
                V.scalar_tensor_tensor(out=shf[:, :], in0=mv[:, :, 0], scalar=-1.0, in1=rs[:, :], op0=ALU.mult, op1=ALU.mult)\
                 .then_inc(shift_ready, 1)

            row_moments(1)
            negated_shift(1)
            dve.wait_ge(xb_ready, 1)
            for c, (c0, cw) in enumerate(CH):
                n0, n1 = c0 // P, (c0 + cw) // P
                dve.wait_ge(y_normed, n1)
                y_ = yr[:, n0:n1, :]
                dl.link(V.tensor_tensor(y_, y_, lnw[:, 0:1, :].to_broadcast([P, n1 - n0, D]), ALU.mult))
                dl.link(V.tensor_tensor(y_, y_, xr[:, n0:n1, :], ALU.add))
                for n in range(n0, n1):
                    V.bn_stats(bst[:, n, :], yr[:, n, :]).then_inc(stat_done, 1)
            row_moments(2)
            negated_shift(2)

            for l in range(3):
                for c, (c0, cw) in enumerate(CH):
                    if l == 0:
                        dve.wait_ge(x1_turned, c + 1)
                        V.tensor_copy(big[:, c0:c0 + cw], bank[c % 2][:, 0:cw]).then_inc(dinv_ready, 1)
                        dve.wait_ge(dinv_ready, c + 1)
                        V.tensor_tensor(acc[:, c0:c0 + cw], bank[2 + c % 2][:, 0:cw], big[:, c0:c0 + cw], ALU.mult).then_inc(acc_set, 1)
                    else:
                        dve.wait_ge(act_ready, NCH * (l - 1) + c + 1)
                        V.tensor_tensor(acc[:, c0:c0 + cw], hd[:, c0:c0 + cw], big[:, c0:c0 + cw], ALU.mult).then_inc(acc_set, 1)
                dve.wait_ge(rows_turned, NCH * (l + 1))
                dve.wait_ge(acc_set, NCH * (l + 1))

                def weigh(B, b, g, s):
                    if s == 0 and not (isinstance(B, int) and NG * B + g < NG):
                        dve.wait_ge(sum_done, NG * B + g - 3)
                    t_ = b * TPB + (g * GRP + s)
                    V.tensor_scalar(oh[:, g, s, :], iota_j[:, :], rel_c[:, bass.ds(t_, 1)], ew_c[:, bass.ds(t_, 1)],
                                    ALU.is_equal, ALU.mult).then_inc(wt_ready, 1)

                def windows(b, i, par, peeled):
                    B = b + NB * l
                    last = isinstance(b, int) and b == NB - 1
                    for g in range(NG):
                        firsts = load_starts(mybir.EngineType.DVE, b * TPB + g * GRP)
                        for s in range(GRP):
                            if g < 2:
                                weigh(B, b, g + 2, s)
                            elif not last:
                                weigh(B + 1, b + 1, g - 2, s)
                            t = g * GRP + s
                            if s == 0:
                                dve.wait_ge(sum_done, NG * B + g + 1)
                            if not (isinstance(B, int) and B == 0 and t == 0):
                                dve.wait_ge(win_added, TPB * B + t)
                            w_ = acc[:, bass.ds(firsts[s], P)]
                            V.tensor_tensor(w_, w_, bank[g][:, s * P:(s + 1) * P], ALU.add).then_inc(win_added, 1)
                for g in range(2):
                    for s in range(GRP):
                        weigh(NB * l, 0, g, s)
                steps_by_pairs(dve, 0, NB, windows, tail=2)

                for c, (c0, cw) in enumerate(CH):
                    dve.wait_ge(lin_done, NCH * l + c + 1)
                    V.tensor_tensor(hd[:, c0:c0 + cw], bank[c % 4][:, 0:cw], big[:, c0:c0 + cw], ALU.mult).then_inc(h_scaled, 1)
                for c, (c0, cw) in enumerate(CH):
                    dve.wait_ge(h_ready, NCH * l + c + 1)
                    dl.inc(V.bn_stats(bst[:, c, :], hd[:, c0:min(c0 + cw, N)]))
                dl.wait()
                V.bn_aggr(mv[:, 0, :], bst[:, 0:NCH, :].rearrange("p c s -> p (c s)")).then_inc(var_ready, 1)
                dve.wait_ge(std_ready, 3 + l)
                dl.link(V.reciprocal(rs[:, 0:1], rs[:, 0:1]))
                dl.link(V.tensor_tensor(bn[:, 0:1], rs[:, 0:1], gcnv[:, 3 + l:4 + l], ALU.mult))
                dl.link(V.tensor_tensor(bn[:, 2:3], mv[:, 0, 0:1], bn[:, 0:1], ALU.mult))
                V.tensor_tensor(bn[:, 1:2], gcnv[:, 6 + l:7 + l], bn[:, 2:3], ALU.subtract).then_inc(bn_ready, 1)

            for c, (c0, cw) in enumerate(CH):
                dve.wait_ge(h_turned, c + 1)
                x_ = xr[:, c0 // P:(c0 + cw) // P, :]
                V.tensor_tensor(x_, x_, bank[4 + c % 4][:, 0:cw].rearrange("p (t f) -> p t f", f=D), ALU.add).then_inc(res_added, 1)
            dve.wait_ge(res_added, NCH)
            with dve.Fori(0, NT) as n:
                V.bn_stats(bst[:, bass.ds(n, 1), :].rearrange("p a s -> p (a s)"),
                           xr[:, bass.ds(n, 1), :].rearrange("p a f -> p (a f)")).then_inc(stat_done, 1)
            row_moments(3)
            with dve.Fori(0, NT) as n:
                x_ = xr[:, bass.ds(n, 1), :].rearrange("p a f -> p (a f)")
                V.tensor_scalar(x_, x_, mv[:, bass.ds(n, 1), 0], rs[:, bass.ds(n, 1)], ALU.subtract, ALU.mult)\
                 .then_inc(out_ready, 1)
    return nc


_INS = ["x", "src", "dst", "edge_type_6", "edge_weight", "node_type_4", "L0_gnn_Wk", "L0_gnn_Wq", "L0_gnn_Wv",
        "L0_gnn_Wa", "L0_gnn_rel_pri", "L0_gnn_rel_att", "L0_gnn_rel_msg", "L0_gnn_skip", "L0_gnn_ln_gamma",
        "L0_gnn_ln_beta", "L1_gnn_W1", "L1_gnn_b1", "L1_gnn_W2", "L1_gnn_b2", "L1_gnn_W3", "L1_gnn_b3",
        "L1_gnn_g1", "L1_gnn_be1", "L1_gnn_g2", "L1_gnn_be2", "L1_gnn_g3", "L1_gnn_be3"]


def kernel(**inputs):
    import numpy as _np
    import concourse.bacc as _bacc
    from concourse import mybir as _mybir
    from concourse.bass_utils import run_bass_kernel_spmd as _run

    nc = _bacc.Bacc("TRN2", target_bir_lowering=False, num_devices=1)
    arrays, args = {}, []
    for name in _INS:
        a = _np.ascontiguousarray(inputs[name])
        arrays[f"in_{name}"] = a
        args.append(nc.dram_tensor(f"in_{name}", a.shape, _mybir.dt.from_np(a.dtype), kind="ExternalInput").ap())
    shape = arrays["in_x"].shape
    args.append(nc.dram_tensor("out_0", shape, _mybir.dt.from_np(_np.dtype("float32")), kind="ExternalOutput").ap())
    gnn(nc, *args)
    r = _run(nc, [arrays], core_ids=[0])
    return r.results[0]["out_0"]
```
